# Optimizing a Trainium2 kernel written in Bass

```python
import numpy as np
import jax
import jax.numpy as jnp

def _softmax(x, axis=-1):
    return jax.nn.softmax(x, axis=axis)

def _gelu(x):
    return jax.nn.gelu(x, approximate=True)

def _silu(x):
    return jax.nn.silu(x)

def _sigmoid(x):
    return jax.nn.sigmoid(x)

def _layernorm(x, axis=-1, eps=1e-05):
    m = jnp.mean(x, axis=axis, keepdims=True)
    v = jnp.var(x, axis=axis, keepdims=True)
    return (x - m) / jnp.sqrt(v + eps)

def _scatter_add(tgt, idx, src, axis=0):
    return tgt.at[idx].add(src)

def _segment_sum(src, seg, n):
    return jax.ops.segment_sum(src, seg, n)
kernel_name = 'mk_gnn_resnorm_d1_gnn_r64_162c45'

def setup_inputs(seed: int=0):
    np.random.seed(seed)
    _w = jnp.asarray

    def _rec_inputs():
        import jax
        import jax.numpy as jnp
        _gk = jax.random.key(seed)
        x = -0.0003713 + 1 * jax.random.normal(jax.random.fold_in(_gk, 1), (100000, 128), jnp.float32)
        src = jax.random.randint(jax.random.fold_in(_gk, 2), (50000,), 0, 100000, jnp.int32)
        dst = jax.random.randint(jax.random.fold_in(_gk, 3), (50000,), 0, 100000, jnp.int32)
        _o = jnp.argsort(dst, stable=True)
        src = src[_o]
        dst = dst[_o]
        edge_weight = jax.random.uniform(jax.random.fold_in(_gk, 12), (50000,), jnp.float32, 0.0, 1)
        return (x, src, dst, edge_weight)
    x, src, dst, edge_weight = _rec_inputs()

    def _L0_gnn_setup():
        import jax, jax.numpy as jnp
        import numpy as np
        N = 100000
        E = 12500
        D = 128
        key = jax.random.key(seed)
        ks = jax.random.split(key, 12)
        s = lambda fan_in: 1.0 / np.sqrt(fan_in)
        return {'h': jax.random.normal(ks[0], (N, D), dtype=jnp.float32), 'w': jax.random.uniform(ks[1], (E,), dtype=jnp.float32), 'src': jax.random.randint(ks[2], (E,), 0, N, dtype=jnp.int32), 'dst': jax.random.randint(ks[3], (E,), 0, N, dtype=jnp.int32), 'W1': jax.random.uniform(ks[4], (2 * D + 1, D), jnp.float32, -s(2 * D + 1), s(2 * D + 1)), 'b1': jnp.zeros((D,), jnp.float32), 'W2': jax.random.uniform(ks[5], (D, D), jnp.float32, -s(D), s(D)), 'b2': jnp.zeros((D,), jnp.float32), 'U1': jax.random.uniform(ks[6], (2 * D, D), jnp.float32, -s(2 * D), s(2 * D)), 'c1': jnp.zeros((D,), jnp.float32), 'U2': jax.random.uniform(ks[7], (D, D), jnp.float32, -s(D), s(D)), 'c2': jnp.zeros((D,), jnp.float32)}
    _L0_gnn_all = _L0_gnn_setup()
    _L0_gnn_in = {k: v for k, v in _L0_gnn_all.items() if k in ('W1', 'b1', 'W2', 'b2', 'U1', 'c1', 'U2', 'c2')}
    del _L0_gnn_all
    return {'x': x, 'src': src, 'dst': dst, 'edge_weight': edge_weight, 'L0_gnn_W1': _L0_gnn_in['W1'], 'L0_gnn_b1': _L0_gnn_in['b1'], 'L0_gnn_W2': _L0_gnn_in['W2'], 'L0_gnn_b2': _L0_gnn_in['b2'], 'L0_gnn_U1': _L0_gnn_in['U1'], 'L0_gnn_c1': _L0_gnn_in['c1'], 'L0_gnn_U2': _L0_gnn_in['U2'], 'L0_gnn_c2': _L0_gnn_in['c2']}

def reference(x, src, dst, edge_weight, L0_gnn_W1, L0_gnn_b1, L0_gnn_W2, L0_gnn_b2, L0_gnn_U1, L0_gnn_c1, L0_gnn_U2, L0_gnn_c2):
    import jax
    import jax.numpy as jnp

    def _L0_gnn_ref(h, w, src, dst, W1, b1, W2, b2, U1, c1, U2, c2):
        import jax, jax.numpy as jnp
        import numpy as np
        N = 100000
        E = 12500
        D = 128
        n = h.shape[0]
        msg_in = jnp.concatenate([h[src], h[dst], w[:, None]], axis=1)
        msg = jax.nn.relu(msg_in @ W1 + b1) @ W2 + b2
        agg = jax.ops.segment_max(msg, dst, num_segments=n)
        deg = jax.ops.segment_sum(jnp.ones((dst.shape[0],), jnp.int32), dst, num_segments=n)
        agg = jnp.where((deg > 0)[:, None], agg, jnp.zeros((), h.dtype))
        upd_in = jnp.concatenate([h, agg], axis=1)
        return jax.nn.relu(upd_in @ U1 + c1) @ U2 + c2
    x = _layernorm(x + _L0_gnn_ref(x, edge_weight, src, dst, L0_gnn_W1, L0_gnn_b1, L0_gnn_W2, L0_gnn_b2, L0_gnn_U1, L0_gnn_c1, L0_gnn_U2, L0_gnn_c2), axis=-1)
    return x

_drawn_inputs = setup_inputs


def setup_inputs(seed=0):
    import zlib

    import numpy as np

    out = dict(_drawn_inputs(seed))
    spreads = {'L0_gnn_b1': (0.0, 2.0),
     'L0_gnn_b2': (0.0, 0.725),
     'L0_gnn_c1': (0.0, 0.1),
     'L0_gnn_c2': (0.0, 0.1)}
    factors = {'edge_weight': 48.452, 'L0_gnn_W1': 2.964}
    for name, (base, spread) in spreads.items():
        noise = np.random.default_rng([zlib.crc32(name.encode()), seed]).standard_normal(out[name].shape)
        drawn = base * np.exp(spread * noise) if base else spread * noise
        out[name] = jnp.asarray(drawn.astype(out[name].dtype))
    for name, factor in factors.items():
        out[name] = (out[name] * factor).astype(out[name].dtype)
    return out
```

```python
import numpy as np
import concourse.bass as bass
from concourse import mybir
from contextlib import ExitStack

P = 128


def build(nc, x, src, dst, edge_weight, W1, b1, W2, b2, U1, c1, U2, c2, out):
    f32, bf16, i32 = mybir.dt.float32, mybir.dt.bfloat16, mybir.dt.int32
    ALU, ACT = mybir.AluOpType, mybir.ActivationFunctionType
    ds = bass.ds

    N, D = x.shape
    E = src.shape[0]
    assert D == P
    EB = 512
    G = EB // P
    STEPS = -(-E // EB)
    NB = 2 * EB
    assert -(-N // NB) == STEPS
    RING = 4
    ROUNDS = STEPS // RING
    LEFT = STEPS - ROUNDS * RING
    assert 1 <= LEFT < RING
    CH = -(-E // (P * P))
    EP = CH * P * P
    FULL = E // P
    REST = E - FULL * P
    CF = FULL // P
    RF = FULL - CF * P
    SKIP = 1 << 20
    NEG = -3.0e38
    EPS = 1e-5

    with ExitStack() as ctx:
        def sb(name, shape, dt=f32):
            return ctx.enter_context(nc.sbuf_tensor(name, shape, dt))

        def sem(name):
            return ctx.enter_context(nc.semaphore(name))

        mask_d = nc.dram_tensor("mask_d", (EP,), bf16).ap()
        wpart_d = nc.dram_tensor("wpart_d", (9, EP), bf16).ap()
        last_d = nc.dram_tensor("last_d", (STEPS, P, G * D), f32).ap()

        w1a, w1b, w2 = sb("w1a", [P, D]), sb("w1b", [P, D]), sb("w2", [P, D])
        u1a, u1b, u2 = sb("u1a", [P, D]), sb("u1b", [P, D]), sb("u2", [P, D])
        b1c, b2c, c1c, c1e, eps = (sb(n, [P, 1]) for n in ("b1c", "b2c", "c1c", "c1e", "eps"))
        ident = sb("ident", [P, P])
        row2 = sb("row2", [1, 2, D])
        part2 = sb("part2", [1, 3, 2, D], bf16)
        c2rep = sb("c2rep", [1, 3, G, D], bf16)
        wc9 = sb("wc9", [P, D], bf16)
        c23 = sb("c23", [P, G * D], bf16)
        ones = sb("ones", [P, P], bf16)

        ints = sb("ints", [P, 4, CH, P], i32)
        wrow = sb("wrow", [P, CH, P])
        srcf, dstf, lastf, scf = (sb(n, [P, CH * P]) for n in ("srcf", "dstf", "lastf", "scf"))
        maskr = sb("maskr", [P, CH, P], bf16)
        wp = sb("wp", [P, 3, CH, P], bf16)
        src_t, dst_t, sc_t = (sb(n, [P, CH * P], i32) for n in ("src_t", "dst_t", "sc_t"))

        gi = sb("gi", [P, RING, 2, G], i32)
        si = sb("si", [P, RING, G], i32)
        xs = sb("xs", [P, RING, G, D])
        xd = sb("xd", [P, RING, G, D])
        mk = sb("mk", [P, RING, EB], bf16)
        w9 = sb("w9", [P, RING, EB], bf16)
        xn = sb("xn", [P, RING, 2 * G, D])
        on = sb("on", [P, RING, 2 * G, D])
        oe = sb("oe", [P, RING, G, D])
        rs = sb("rs", [P, RING, G, D])

        xsT, xdT, h1, h2 = (sb(n, [P, EB]) for n in ("xsT", "xdT", "h1", "h2"))
        agg = sb("agg", [P, 2, EB])
        xnT = sb("xnT", [P, 2, EB])
        hn = sb("hn", [P, 2, EB])
        stats = sb("stats", [P, 3, G, 6])
        mv = sb("mv", [P, 3, G, 2])
        std = sb("std", [P, 3, G])
        rstd = sb("rstd", [P, 3, G])

        def bank(name):
            return ctx.enter_context(nc.psum_tensor(name, [P, EB], f32))

        pXs = bank("pXs")
        pXdH = bank("pXdH")
        pMU = bank("pMU")
        pZe = bank("pZe")
        pXn = bank("pXn")
        pHn = bank("pHn")
        pZn = [bank("pZn0"), bank("pZn1")]

        zeroed = sem("zeroed")
        ident_ok = sem("ident_ok")
        weights_in = sem("weights_in")
        rows_in = sem("rows_in")
        ints_in = sem("ints_in")
        chain = sem("chain")
        indices_ok = sem("indices_ok")
        scratch_ok = sem("scratch_ok")
        parts_ok = sem("parts_ok")
        parts_in = sem("parts_in")
        scratch_out = sem("scratch_out")
        tables_T = sem("tables_T")
        b2u_done = sem("b2u_done")
        tables_ok = sem("tables_ok")
        c1e_ok = sem("c1e_ok")
        xn_in = [sem(f"xn_in{k}") for k in range(RING)]
        aux_in = [sem(f"aux_in{k}") for k in range(RING)]
        gathered = [sem(f"gathered{k}") for k in range(RING)]
        on_out = [sem(f"on_out{k}") for k in range(RING)]
        oe_out = [sem(f"oe_out{k}") for k in range(RING)]
        gi_ok = sem("gi_ok")
        si_ok = sem("si_ok")
        e_xT = sem("e_xT")
        e_h1 = sem("e_h1")
        e_msg = sem("e_msg")
        e_h2 = sem("e_h2")
        e_z = sem("e_z")
        n_xT = sem("n_xT")
        n_h = sem("n_h")
        n_z = sem("n_z")
        xsT_ok, xdT_ok = sem("xsT_ok"), sem("xdT_ok")
        h1_ok, h2_ok = sem("h1_ok"), sem("h2_ok")
        xnT_ok, hn_ok = sem("xnT_ok"), sem("hn_ok")
        agg_ok = sem("agg_ok")
        added = sem("added")
        stat_ok = sem("stat_ok")
        var_ok = sem("var_ok")
        std_ok = sem("std_ok")
        rstd_ok = sem("rstd_ok")
        norm_ok = sem("norm_ok")
        rs_in = [sem(f"rs_in{k}") for k in range(RING)]
        scattered = [sem(f"scattered{k}") for k in range(RING)]

        NW = 10
        block = ctx.enter_context(nc.Block())

        @block.sync
        def _(sp):
            sp.wait_ge(zeroed, 1)
            cr = "(c r l) -> r c l"
            for k, (a, off) in enumerate(((src, 0), (dst, 0), (dst, -1), (dst, 1))):
                c0 = 1 if off < 0 else 0
                sp.dma_start(ints[:, k, c0:CF, :],
                             a[c0 * P * P + off:CF * P * P + off].rearrange(cr, r=P, l=P)).then_inc(ints_in, 16)
                sp.dma_start(ints[0:RF, k, CF, :],
                             a[CF * P * P + off:FULL * P + off].rearrange("(r l) -> r l", l=P)).then_inc(ints_in, 16)
                n = REST - 1 if off > 0 else REST
                sp.dma_start(ints[RF:RF + 1, k, CF, 0:n],
                             a[FULL * P + off:FULL * P + off + n].rearrange("(r l) -> r l", r=1)).then_inc(ints_in, 16)
            sp.dma_start(ints[1:P, 2, 0, :],
                         dst[P - 1:P * P - 1].rearrange("(r l) -> r l", l=P)).then_inc(ints_in, 16)
            sp.dma_start(ints[0:1, 2, 0, 1:P], dst[0:P - 1].rearrange("(r l) -> r l", r=1)).then_inc(ints_in, 16)
            sp.dma_start(wrow[:, 0:CF, :], edge_weight[0:CF * P * P].rearrange(cr, r=P, l=P)).then_inc(ints_in, 16)
            sp.dma_start(wrow[0:RF, CF, :],
                         edge_weight[CF * P * P:FULL * P].rearrange("(r l) -> r l", l=P)).then_inc(ints_in, 16)
            sp.dma_start(wrow[RF:RF + 1, CF, 0:REST],
                         edge_weight[FULL * P:E].rearrange("(r l) -> r l", r=1)).then_inc(ints_in, 16)

            def first_node(i, u):
                last = isinstance(i, int) and RING * i + u == STEPS - 1
                return N - NB if last else (RING * i + u) * NB

            def node_load(i, u, reused):
                k, step = u, RING * i + u
                if reused:
                    sp.wait_ge(added, 3 * (step - RING) + 2)
                sp.dma_start(xn[:, k], x[ds(first_node(i, u), NB), :].rearrange("(p g) d -> p g d", p=P)
                             ).then_inc(xn_in[k], 16)

            def aux_load(i, u, reused):
                k, step = u, RING * i + u
                if reused:
                    sp.wait_ge(agg_ok, step - RING + 1)
                sp.dma_start(mk[:, k], mask_d[ds(step * EB, EB)].rearrange("(a e) -> a e", a=1)
                             .broadcast_to([P, EB])).then_inc(aux_in[k], 16)
                sp.dma_start(w9[0:9, k], wpart_d[:, ds(step * EB, EB)]).then_inc(aux_in[k], 16)

            def stores(i, u):
                k, step = u, RING * i + u
                sp.wait_ge(norm_ok, 3 * step + 3)
                if isinstance(step, int) and step == STEPS - 1:
                    for j in range(RING):
                        sp.wait_ge(on_out[j], 16 * (ROUNDS + (j < LEFT - 1)))
                sp.dma_start(out[ds(first_node(i, u), NB), :].rearrange("(p g) d -> p g d", p=P), on[:, k]
                             ).then_inc(on_out[k], 16)
                sp.dma_start(last_d[ds(step, 1)].rearrange("a p f -> (a p) f"),
                             oe[:, k].rearrange("p g d -> p (g d)")).then_inc(oe_out[k], 16)

            node_load(0, 0, False)
            node_load(0, 1, False)
            sp.wait_ge(scratch_out, 16 * 10)
            aux_load(0, 0, False)
            aux_load(0, 1, False)

            def step_of(i, u, reused):
                j, v = i + (u + 2) // RING, (u + 2) % RING
                if not (isinstance(i, int) and RING * j + v >= STEPS):
                    node_load(j, v, reused)
                    aux_load(j, v, reused)
                stores(i, u)

            for u in range(RING):
                step_of(0, u, u + 2 >= RING)
            with sp.Fori(1, ROUNDS - 1) as i:
                for u in range(RING):
                    step_of(i, u, True)
            for u in range(RING):
                step_of(ROUNDS - 1, u, True)
            for u in range(LEFT):
                step_of(ROUNDS, u, True)

            for j in range(RING):
                sp.wait_ge(oe_out[j], 16 * (ROUNDS + (j < LEFT)))

            def row_load(i, u, reused):
                if reused:
                    sp.wait_ge(scattered[u], 16 * G * i)
                sp.dma_start(rs[:, u].rearrange("p g d -> p (g d)"),
                             last_d[ds(RING * i + u, 1)].rearrange("a p f -> (a p) f")).then_inc(rs_in[u], 16)

            for u in range(RING):
                row_load(0, u, False)
            with sp.Fori(1, ROUNDS) as i:
                for u in range(RING):
                    row_load(i, u, True)
            for u in range(LEFT):
                row_load(ROUNDS, u, True)
            for j in range(RING):
                sp.wait_ge(scattered[j], 16 * G * (ROUNDS + (j < LEFT)))

        @block.gpsimd
        def _(pool):
            pool.memset(ident[:, :], 0.0).then_inc(ident_ok, 1)
            pool.wait_ge(ident_ok, 1)
            pool.affine_select(out=ident[:, :], in_=ident[:, :], compare_op=ALU.not_equal, fill=1.0, base=0,
                               pattern=[[-1, P]], channel_multiplier=1).then_inc(ident_ok, 1)

            def gathers(i, u, reused):
                step = RING * i + u
                pool.wait_ge(gi_ok, step + 1)
                if reused:
                    pool.wait_ge(e_xT, step - RING + 1)
                pool.nop(nofuse=True)
                for j in range(G):
                    pool.indirect_dma_start(xs[:, u, j, :], None, x[:, :],
                                            bass.IndirectOffsetOnAxis(ap=gi[:, u, 0, j:j + 1], axis=0)
                                            ).then_inc(gathered[u], 16)
                if reused:
                    pool.wait_ge(added, 3 * (step - RING) + 3)
                    pool.nop(nofuse=True)
                for j in range(G):
                    pool.indirect_dma_start(xd[:, u, j, :], None, x[:, :],
                                            bass.IndirectOffsetOnAxis(ap=gi[:, u, 1, j:j + 1], axis=0)
                                            ).then_inc(gathered[u], 16)

            for u in range(RING):
                gathers(0, u, False)
            with pool.Fori(1, ROUNDS) as i:
                for u in range(RING):
                    gathers(i, u, True)
            for u in range(LEFT):
                gathers(ROUNDS, u, True)

            for j in range(RING):
                pool.wait_ge(on_out[j], 16 * (ROUNDS + (j < LEFT)))

            def scatters(i, u):
                pool.wait_ge(si_ok, RING * i + u + 1)
                pool.wait_ge(rs_in[u], 16 * (i + 1))
                pool.nop(nofuse=True)
                for j in range(G):
                    pool.indirect_dma_start(out[:, :], bass.IndirectOffsetOnAxis(ap=si[:, u, j:j + 1], axis=0),
                                            rs[:, u, j, :], None, bounds_check=N - 1, oob_is_err=False
                                            ).then_inc(scattered[u], 16)

            for u in range(RING):
                scatters(0, u)
            with pool.Fori(1, ROUNDS) as i:
                for u in range(RING):
                    scatters(i, u)
            for u in range(LEFT):
                scatters(ROUNDS, u)
            for j in range(RING):
                pool.wait_ge(scattered[j], 16 * G * (ROUNDS + (j < LEFT)))

        @block.tensor
        def _(pe):
            pe.wait_ge(weights_in, 16 * NW)
            nc.tensor.matmul(pZe[:, 0:1], u1b[:, :], b2c[:, :], start=True, stop=True).then_inc(b2u_done, 1)
            pe.wait_ge(ident_ok, 2)
            pe.wait_ge(indices_ok, 1)
            for bk, t in ((pXs, srcf), (pXdH, dstf), (pMU, scf)):
                for c in range(CH):
                    nc.tensor.transpose(bk[:, c * P:(c + 1) * P], t[:, c * P:(c + 1) * P], ident[:, :]
                                        ).then_inc(tables_T, 1)
            pe.wait_ge(zeroed, 1)
            pe.wait_ge(tables_ok, 3)

            def transpose_edges(i, u):
                pe.wait_ge(gathered[u], 16 * 2 * G * (i + 1))
                for bk, t in ((pXs, xs), (pXdH, xd)):
                    for j in range(G):
                        last = nc.tensor.transpose(bk[:, j * P:(j + 1) * P], t[:, u, j, :], ident[:, :])
                last.then_inc(e_xT, 1)

            def transpose_nodes(i, u, b):
                if b == 0:
                    pe.wait_ge(xn_in[u], 16 * (i + 1))
                else:
                    pe.wait_ge(xnT_ok, 2 * (RING * i + u) + 1)
                for j in range(G):
                    last = nc.tensor.transpose(pXn[:, j * P:(j + 1) * P], xn[:, u, b * G + j, :], ident[:, :])
                last.then_inc(n_xT, 1)

            def message_hidden(i, u):
                step = RING * i + u
                pe.wait_ge(aux_in[u], 32 * (i + 1))
                pe.wait_ge(xsT_ok, step + 1)
                pe.wait_ge(xdT_ok, step + 1)
                nc.tensor.matmul(pXdH[:, :], wc9[:, :], w9[:, u, :], start=True, stop=False)
                nc.tensor.matmul(pXdH[:, :], w1a[:, :], xsT[:, :], start=False, stop=False)
                nc.tensor.matmul(pXdH[:, :], w1b[:, :], xdT[:, :], start=False, stop=True).then_inc(e_h1, 1)

            def messages(i, u):
                pe.wait_ge(h1_ok, RING * i + u + 1)
                nc.tensor.matmul(pMU[:, :], w2[:, :], h1[:, :], start=True, stop=True).then_inc(e_msg, 1)

            def update_hidden(i, u):
                pe.wait_ge(agg_ok, RING * i + u + 1)
                nc.tensor.matmul(pMU[:, :], u1a[:, :], xdT[:, :], start=True, stop=False)
                nc.tensor.matmul(pMU[:, :], u1b[:, :], agg[:, u % 2, :], start=False, stop=True).then_inc(e_h2, 1)

            def updates(bk, hT, done):
                nc.tensor.matmul(bk[:, :], ones[:, :], c23[:, :], start=True, stop=False)
                for j in range(G):
                    last = nc.tensor.matmul(bk[:, j * P:(j + 1) * P], hT[:, j * P:(j + 1) * P], u2[:, :],
                                            start=False, stop=(j == G - 1))
                last.then_inc(done, 1)

            def node_hidden(i, u, b):
                pe.wait_ge(xnT_ok, 2 * (RING * i + u) + b + 1)
                nc.tensor.matmul(pHn[:, :], u1a[:, :], xnT[:, b, :], start=True, stop=True).then_inc(n_h, 1)

            def node_updates(i, u, b, first):
                step = RING * i + u
                pe.wait_ge(hn_ok, 2 * step + b + 1)
                if not first:
                    pe.wait_ge(added, 3 * (step - 1) + b + 1)
                updates(pZn[b], hn[:, b, :], n_z)

            def edge_updates(i, u, first):
                step = RING * i + u
                pe.wait_ge(h2_ok, step + 1)
                if not first:
                    pe.wait_ge(added, 3 * (step - 1) + 3)
                updates(pZe, h2[:, :], e_z)

            def step_of(i, u, first=False, last=False):
                j, v = i + (u + 1) // RING, (u + 1) % RING
                message_hidden(i, u)
                transpose_nodes(i, u, 1)
                node_hidden(i, u, 0)
                messages(i, u)
                node_updates(i, u, 0, first)
                node_hidden(i, u, 1)
                update_hidden(i, u)
                node_updates(i, u, 1, first)
                if not last:
                    transpose_edges(j, v)
                    transpose_nodes(j, v, 0)
                edge_updates(i, u, first)

            pe.wait_ge(c1e_ok, 1)
            pe.wait_ge(parts_in, 16 * 12)
            transpose_edges(0, 0)
            transpose_nodes(0, 0, 0)
            for u in range(RING):
                step_of(0, u, first=(u == 0))
            with pe.Fori(1, ROUNDS) as i:
                for u in range(RING):
                    step_of(i, u)
            for u in range(LEFT):
                step_of(ROUNDS, u, last=(u == LEFT - 1))

        @block.scalar
        def _(act):
            act.dma_start(row2[0:1, 0, :], W1[2 * D:2 * D + 1, :]).then_inc(rows_in, 16)
            act.dma_start(row2[0:1, 1, :], c2.rearrange("(a d) -> a d", a=1)).then_inc(rows_in, 16)
            for t, a in ((w1a, W1[0:D, :]), (w1b, W1[D:2 * D, :]), (w2, W2[:, :]), (u1a, U1[0:D, :]),
                         (u1b, U1[D:2 * D, :]), (u2, U2[:, :])):
                act.dma_start(t[:, :], a).then_inc(weights_in, 16)
            for t, a in ((b1c, b1), (b2c, b2), (c1c, c1)):
                act.dma_start(t[:, :], a.rearrange("(d a) -> d a", a=1)).then_inc(weights_in, 16)
            act.dma_start(c1e[:, :], c1.rearrange("(d a) -> d a", a=1)).then_inc(weights_in, 16)
            act.wait_ge(parts_ok, 1)
            for c in range(3):
                for a in range(3):
                    act.dma_start(wc9[3 * c + a:3 * c + a + 1, :], part2[0:1, c, 0, :]).then_inc(parts_in, 16)
                act.dma_start(c23[c:c + 1, :], c2rep[0:1, c].rearrange("p g d -> p (g d)")).then_inc(parts_in, 16)
            act.wait_ge(scratch_ok, 1)
            cr = "(c r l) -> r c l"
            act.dma_start(mask_d.rearrange(cr, r=P, l=P), maskr[:, :, :]).then_inc(scratch_out, 16)
            for c in range(3):
                for a in range(3):
                    act.dma_start(wpart_d[3 * c + a].rearrange(cr, r=P, l=P), wp[:, a]).then_inc(scratch_out, 16)

            def gather_rows(i, u, reused):
                if reused:
                    act.wait_ge(gathered[u], 16 * 2 * G * i)
                col = (RING * i + u) * G
                nc.scalar.copy(gi[:, u, 0, :], src_t[:, ds(col, G)])
                nc.scalar.copy(gi[:, u, 1, :], dst_t[:, ds(col, G)]).then_inc(gi_ok, 1)

            act.wait_ge(tables_ok, 3)
            for u in range(RING):
                gather_rows(0, u, False)
            act.wait_ge(c1e_ok, 1)
            act.wait_ge(weights_in, 16 * NW)

            def edge_rows_T(i, u):
                step = RING * i + u
                act.wait_ge(e_xT, step + 1)
                nc.scalar.copy(xsT[:, :], pXs[:, :]).then_inc(xsT_ok, 1)
                nc.scalar.copy(xdT[:, :], pXdH[:, :]).then_inc(xdT_ok, 1)

            def node_rows_T(i, u, b):
                act.wait_ge(n_xT, 2 * (RING * i + u) + b + 1)
                nc.scalar.copy(xnT[:, b, :], pXn[:, :]).then_inc(xnT_ok, 1)

            def node_relu(i, u, b):
                act.wait_ge(n_h, 2 * (RING * i + u) + b + 1)
                nc.scalar.activation(hn[:, b, :], pHn[:, :], ACT.Relu, bias=c1c[:, :]).then_inc(hn_ok, 1)

            def root(i, u, b):
                act.wait_ge(var_ok, 3 * (RING * i + u) + b + 1)
                nc.scalar.activation(std[:, b, :], mv[:, b, :, 1], ACT.Sqrt, bias=eps[:, :]).then_inc(std_ok, 1)

            def step_of(i, u, last=False, copies=True):
                step = RING * i + u
                j, v = i + (u + 1) // RING, (u + 1) % RING
                act.wait_ge(e_h1, step + 1)
                nc.scalar.activation(h1[:, :], pXdH[:, :], ACT.Relu, bias=b1c[:, :]).then_inc(h1_ok, 1)
                node_rows_T(i, u, 1)
                node_relu(i, u, 0)
                node_relu(i, u, 1)
                root(i, u, 0)
                act.wait_ge(e_h2, step + 1)
                nc.scalar.activation(h2[:, :], pMU[:, :], ACT.Relu, bias=c1e[:, :]).then_inc(h2_ok, 1)
                if not last:
                    edge_rows_T(j, v)
                    node_rows_T(j, v, 0)
                if copies:
                    gather_rows(i + 1, u, True)
                root(i, u, 1)
                root(i, u, 2)

            edge_rows_T(0, 0)
            node_rows_T(0, 0, 0)
            for u in range(RING):
                step_of(0, u)
            with act.Fori(1, ROUNDS - 1) as i:
                for u in range(RING):
                    step_of(i, u)
            for u in range(RING):
                step_of(ROUNDS - 1, u, copies=(u < LEFT))
            for u in range(LEFT):
                step_of(ROUNDS, u, last=(u == LEFT - 1), copies=False)

            def scatter_rows(i, u, reused):
                if reused:
                    act.wait_ge(scattered[u], 16 * G * i)
                nc.scalar.copy(si[:, u, :], sc_t[:, ds((RING * i + u) * G, G)]).then_inc(si_ok, 1)

            for u in range(RING):
                scatter_rows(0, u, False)
            with act.Fori(1, ROUNDS) as i:
                for u in range(RING):
                    scatter_rows(i, u, True)
            for u in range(LEFT):
                scatter_rows(ROUNDS, u, True)

        @block.vector
        def _(dve):
            links = [0]

            def link(ins):
                links[0] += 1
                ins.then_inc(chain, 1)
                dve.wait_ge(chain, links[0])

            nc.vector.memset(ints[:, 0], 0)
            nc.vector.memset(ints[:, 1:4], -1)
            nc.vector.memset(wrow[:, :, :], 0.0)
            nc.vector.memset(wc9[:, :], 0.0)
            nc.vector.memset(c23[:, :], 0.0)
            nc.vector.memset(w9[:, :, :], 0.0)
            nc.vector.memset(eps[:, :], EPS)
            nc.vector.memset(ones[:, :], 1.0).then_inc(zeroed, 1)
            dve.wait_ge(zeroed, 1)

            def three_parts(part, rest):
                for a in range(3):
                    link(nc.vector.tensor_copy(part[:, a], rest))
                    if a < 2:
                        link(nc.vector.tensor_tensor(rest, rest, part[:, a], ALU.subtract))

            dve.wait_ge(ints_in, 16 * 17)
            flat = [ints[:, k].rearrange("r c l -> r (c l)") for k in range(4)]
            nc.vector.tensor_copy(srcf[:, :], flat[0])
            nc.vector.tensor_scalar(dstf[:, :], flat[1], 0.0, None, ALU.max)
            link(nc.vector.tensor_tensor(lastf[:, :], flat[1], flat[3], ALU.not_equal))
            link(nc.vector.scalar_tensor_tensor(out=scf[:, :], in0=flat[1], scalar=float(-SKIP), in1=lastf[:, :],
                                                op0=ALU.add, op1=ALU.mult))
            nc.vector.tensor_scalar(scf[:, :], scf[:, :], float(SKIP), None, ALU.add).then_inc(indices_ok, 1)
            link(nc.vector.tensor_tensor(lastf[:, :], flat[1], flat[2], ALU.not_equal))
            link(nc.vector.tensor_scalar(maskr[:, :, :].rearrange("r c l -> r (c l)"), lastf[:, :], NEG, None,
                                         ALU.mult))
            three_parts(wp, wrow[:, :, :])
            dve.wait_ge(chain, links[0])
            dve.nop(nofuse=True)
            dve.sem_inc(scratch_ok, 1)
            dve.wait_ge(rows_in, 32)
            three_parts(part2, row2[:, :, :])
            for g in range(G):
                last = nc.vector.tensor_copy(c2rep[:, :, g, :], part2[:, :, 1, :])
            last.then_inc(parts_ok, 1)
            for n, (t, bk) in enumerate(((src_t, pXs), (dst_t, pXdH), (sc_t, pMU))):
                dve.wait_ge(tables_T, CH * (n + 1))
                nc.vector.tensor_copy(t[:, :], bk[:, 0:CH * P]).then_inc(tables_ok, 1)
            dve.wait_ge(b2u_done, 1)
            dve.wait_ge(weights_in, 16 * NW)
            nc.vector.tensor_tensor(c1e[:, :], c1e[:, :], pZe[:, 0:1], ALU.add).then_inc(c1e_ok, 1)

            def running_max(i, u, first=False):
                step = RING * i + u
                dve.wait_ge(e_msg, step + 1)
                if not first:
                    dve.wait_ge(agg_ok, step)
                nc.vector.tensor_tensor_scan(agg[:, u % 2, :], mk[:, u, :], pMU[:, :],
                                             NEG if first else agg[:, (u + 1) % 2, EB - 1:EB],
                                             ALU.add, ALU.max).then_inc(agg_ok, 1)

            def result(u, b):
                if b < 2:
                    return on[:, u, b * G:(b + 1) * G, :], pZn[b], xn[:, u, b * G:(b + 1) * G, :]
                return oe[:, u], pZe, xd[:, u]

            def residual(i, u, b, reused):
                z, bk, rows = result(u, b)
                batch = 3 * (RING * i + u) + b
                if b < 2:
                    dve.wait_ge(n_z, 2 * (RING * i + u) + b + 1)
                else:
                    dve.wait_ge(e_z, RING * i + u + 1)
                if reused and b != 1:
                    dve.wait_ge(on_out[u] if b == 0 else oe_out[u], 16 * i)
                nc.vector.tensor_tensor(z, bk[:, :].rearrange("p (g d) -> p g d", g=G), rows, ALU.add
                                        ).then_inc(added, 1)
                dve.wait_ge(added, batch + 1)
                for g in range(G):
                    last = nc.vector.bn_stats(stats[:, b, g, :], z[:, g, :])
                last.then_inc(stat_ok, 1)
                dve.wait_ge(stat_ok, batch + 1)
                dve.nop(nofuse=True)
                for g in range(G):
                    last = nc.vector.bn_aggr(mv[:, b, g, :], stats[:, b, g, :])
                last.then_inc(var_ok, 1)

            def normalise(i, u, b):
                z, _, _ = result(u, b)
                batch = 3 * (RING * i + u) + b
                dve.wait_ge(std_ok, batch + 1)
                nc.vector.reciprocal(rstd[:, b, :], std[:, b, :]).then_inc(rstd_ok, 1)
                dve.wait_ge(rstd_ok, batch + 1)
                for g in range(G):
                    last = nc.vector.tensor_scalar(z[:, g, :], z[:, g, :], mv[:, b, g, 0:1], rstd[:, b, g:g + 1],
                                                   ALU.subtract, ALU.mult)
                last.then_inc(norm_ok, 1)

            def step_of(i, u, first=False, reused=True):
                running_max(i, u, first)
                residual(i, u, 0, reused)
                residual(i, u, 1, reused)
                normalise(i, u, 0)
                residual(i, u, 2, reused)
                normalise(i, u, 1)
                normalise(i, u, 2)

            for u in range(RING):
                step_of(0, u, first=(u == 0), reused=False)
            with dve.Fori(1, ROUNDS) as i:
                for u in range(RING):
                    step_of(i, u)
            for u in range(LEFT):
                step_of(ROUNDS, u)


_INS = ['x', 'src', 'dst', 'edge_weight', 'L0_gnn_W1', 'L0_gnn_b1', 'L0_gnn_W2', 'L0_gnn_b2',
        'L0_gnn_U1', 'L0_gnn_c1', 'L0_gnn_U2', 'L0_gnn_c2']


def kernel(**inputs):
    import concourse.bacc as _bacc
    from concourse.bass_utils import run_bass_kernel_spmd as _run

    nc = _bacc.Bacc("TRN2", target_bir_lowering=False, num_devices=1)
    arrays, args = {}, []
    for name in _INS:
        a = np.ascontiguousarray(inputs[name])
        arrays[f"in_{name}_dram"] = a
        args.append(nc.dram_tensor(f"in_{name}_dram", a.shape, mybir.dt.from_np(a.dtype), kind="ExternalInput").ap())
    x = inputs['x']
    args.append(nc.dram_tensor("out_0_dram", x.shape, mybir.dt.float32, kind="ExternalOutput").ap())
    build(nc, *args)
    r = _run(nc, [arrays], core_ids=[0])
    return r.results[0]["out_0_dram"]
```

```python
import numpy as np
import concourse.bass as bass
from concourse import mybir
from contextlib import ExitStack

P = 128


def build(nc, x, src, dst, edge_weight, W1, b1, W2, b2, U1, c1, U2, c2, out):
    f32, bf16, i32 = mybir.dt.float32, mybir.dt.bfloat16, mybir.dt.int32
    ALU, ACT = mybir.AluOpType, mybir.ActivationFunctionType
    ds = bass.ds

    N, D = x.shape
    E = src.shape[0]
    assert D == P
    EB = 512
    G = EB // P
    STEPS = -(-E // EB)
    NB = 2 * EB
    assert -(-N // NB) == STEPS
    RING = 4
    LONG = 8
    LAG = LONG - 1
    AHEAD = 2
    LEFT = STEPS % LONG
    ROUNDS = STEPS // LONG
    PE_ROUNDS = STEPS // RING
    assert LONG == 2 * RING and 1 <= LEFT < RING
    CH = -(-E // (P * P))
    EP = CH * P * P
    FULL = E // P
    REST = E - FULL * P
    CF = FULL // P
    RF = FULL - CF * P
    SKIP = 1 << 20
    NEG = -3.0e38
    EPS = 1e-5

    with ExitStack() as ctx:
        def sb(name, shape, dt=f32):
            return ctx.enter_context(nc.sbuf_tensor(name, shape, dt))

        def sem(name):
            return ctx.enter_context(nc.semaphore(name))

        mask_d = nc.dram_tensor("mask_d", (EP,), bf16).ap()
        wpart_d = nc.dram_tensor("wpart_d", (9, EP), bf16).ap()
        src_d, dst_d = (nc.dram_tensor(n, (E, 1), i32).ap() for n in ("src_d", "dst_d"))
        w_d = nc.dram_tensor("w_d", (E, 1), i32).ap()
        last_d = nc.dram_tensor("last_d", (STEPS, P, G * D), f32).ap()

        w1a, w1b, w2 = sb("w1a", [P, D]), sb("w1b", [P, D]), sb("w2", [P, D])
        u1a, u1b, u2 = sb("u1a", [P, D]), sb("u1b", [P, D]), sb("u2", [P, D])
        b1c, b2c, c1c, c1e, eps = (sb(n, [P, 1]) for n in ("b1c", "b2c", "c1c", "c1e", "eps"))
        ident = sb("ident", [P, P])
        row2 = sb("row2", [1, 2, D])
        part2 = sb("part2", [1, 3, 2, D], bf16)
        c2rep = sb("c2rep", [1, 3, G, D], bf16)
        wc9 = sb("wc9", [P, D], bf16)
        c23 = sb("c23", [P, G * D], bf16)
        ones = sb("ones", [P, P], bf16)

        ints = sb("ints", [P, 4, CH, P], i32)
        wrow = sb("wrow", [P, CH, P])
        srcf, dstf, lastf, nowf, latef = (sb(n, [P, CH * P]) for n in ("srcf", "dstf", "lastf", "nowf", "latef"))
        limit = sb("limit", [P, CH * P], i32)
        flagp = sb("flagp", [P, 2])
        ones1 = sb("ones1", [P, 1])
        flags = sb("flags", [1, 2], i32)
        maskr = sb("maskr", [P, CH, P], bf16)
        wp = sb("wp", [P, 3, CH, P], bf16)
        src_t, dst_t, now_t, late_t = (sb(n, [P, CH * P], i32) for n in ("src_t", "dst_t", "now_t", "late_t"))

        CW = E // 16
        assert CW * 16 == E
        chunk = sb("chunk", [P, CW], i32)
        chunk_pos = sb("chunk_pos", [P, CW])
        before = sb("before", [P, CW])
        place = sb("place", [P, CH * P])
        place_i = sb("place_i", [P, CH * P], i32)
        count = sb("count", [P, CH * P])
        rank = sb("rank", [P, CH * P])
        moved = sb("moved", [P, 4], i32)

        gi = sb("gi", [P, RING, 2, G], i32)
        si = sb("si", [P, LONG, G], i32)
        li = sb("li", [P, RING, G], i32)
        xs = sb("xs", [P, RING, G, D])
        xd = sb("xd", [P, RING, G, D])
        mk = sb("mk", [P, RING, EB], bf16)
        w9 = sb("w9", [P, RING, EB], bf16)
        xn = sb("xn", [P, RING, 2 * G, D])
        on = sb("on", [P, RING, 2 * G, D])
        oe = sb("oe", [P, LONG, G, D])
        rs = sb("rs", [P, RING, G, D])

        xsT, xdT, h1, h2 = (sb(n, [P, EB]) for n in ("xsT", "xdT", "h1", "h2"))
        agg = sb("agg", [P, 2, EB])
        xnT = sb("xnT", [P, 2, EB])
        hn = sb("hn", [P, 2, EB])
        stats = sb("stats", [P, 3, G, 6])
        mv = sb("mv", [P, 3, G, 2])
        std = sb("std", [P, 3, G])
        rstd = sb("rstd", [P, 3, G])

        def bank(name):
            return ctx.enter_context(nc.psum_tensor(name, [P, EB], f32))

        pXs = bank("pXs")
        pXdH = bank("pXdH")
        pMU = bank("pMU")
        pZe = bank("pZe")
        pXn = bank("pXn")
        pHn = bank("pHn")
        pZn = [bank("pZn0"), bank("pZn1")]

        zeroed = sem("zeroed")
        ident_ok = sem("ident_ok")
        weights_in = sem("weights_in")
        rows_in = sem("rows_in")
        ints_in = sem("ints_in")
        chain = sem("chain")
        sort_chain = sem("sort_chain")
        indices_ok = sem("indices_ok")
        scratch_ok = sem("scratch_ok")
        parts_ok = sem("parts_ok")
        parts_in = sem("parts_in")
        scratch_out = sem("scratch_out")
        tables_T = sem("tables_T")
        b2u_done = sem("b2u_done")
        tables_ok = sem("tables_ok")
        c1e_ok = sem("c1e_ok")
        xn_in = [sem(f"xn_in{k}") for k in range(RING)]
        aux_in = [sem(f"aux_in{k}") for k in range(RING)]
        gathered = [sem(f"gathered{k}") for k in range(RING)]
        on_out = [sem(f"on_out{k}") for k in range(RING)]
        oe_out = [sem(f"oe_out{k}") for k in range(LONG)]
        gi_ok = sem("gi_ok")
        si_ok = sem("si_ok")
        li_ok = sem("li_ok")
        e_xT = sem("e_xT")
        e_h1 = sem("e_h1")
        e_msg = sem("e_msg")
        e_h2 = sem("e_h2")
        e_z = sem("e_z")
        n_xT = sem("n_xT")
        n_h = sem("n_h")
        n_z = sem("n_z")
        xsT_ok, xdT_ok = sem("xsT_ok"), sem("xdT_ok")
        h1_ok, h2_ok = sem("h1_ok"), sem("h2_ok")
        xnT_ok, hn_ok = sem("xnT_ok"), sem("hn_ok")
        agg_ok = sem("agg_ok")
        added = sem("added")
        stat_ok = sem("stat_ok")
        var_ok = sem("var_ok")
        std_ok = sem("std_ok")
        rstd_ok = sem("rstd_ok")
        norm_ok = sem("norm_ok")
        scattered = [sem(f"scattered{k}") for k in range(LONG)]
        rs_in = [sem(f"rs_in{k}") for k in range(RING)]
        late_out = [sem(f"late_out{k}") for k in range(RING)]
        iota_ok = sem("iota_ok")
        flag_in = sem("flag_in")
        flag_sum = sem("flag_sum")
        flag_ok = sem("flag_ok")
        chunk_free = sem("chunk_free")
        chunk_in = sem("chunk_in")
        compared = sem("compared")
        counted = sem("counted")
        moved_free = sem("moved_free")
        moved_ok = sem("moved_ok")
        moved_out = sem("moved_out")
        sorted_in = sem("sorted_in")

        NW = 10
        block = ctx.enter_context(nc.Block())

        @block.sync
        def _(sp):
            cr = "(c r l) -> r c l"

            def load_edges(src, dst, weight, done):
                for k, (a, off) in enumerate(((src, 0), (dst, 0), (dst, -1), (dst, 1))):
                    c0 = 1 if off < 0 else 0
                    sp.dma_start(ints[:, k, c0:CF, :],
                                 a[c0 * P * P + off:CF * P * P + off].rearrange(cr, r=P, l=P)).then_inc(done, 16)
                    sp.dma_start(ints[0:RF, k, CF, :],
                                 a[CF * P * P + off:FULL * P + off].rearrange("(r l) -> r l", l=P)
                                 ).then_inc(done, 16)
                    n = REST - 1 if off > 0 else REST
                    sp.dma_start(ints[RF:RF + 1, k, CF, 0:n],
                                 a[FULL * P + off:FULL * P + off + n].rearrange("(r l) -> r l", r=1)
                                 ).then_inc(done, 16)
                sp.dma_start(ints[1:P, 2, 0, :],
                             dst[P - 1:P * P - 1].rearrange("(r l) -> r l", l=P)).then_inc(done, 16)
                sp.dma_start(ints[0:1, 2, 0, 1:P], dst[0:P - 1].rearrange("(r l) -> r l", r=1)).then_inc(done, 16)
                wr = wrow[:, :, :].bitcast(i32)
                sp.dma_start(wr[:, 0:CF, :], weight[0:CF * P * P].rearrange(cr, r=P, l=P)).then_inc(done, 16)
                sp.dma_start(wr[0:RF, CF, :],
                             weight[CF * P * P:FULL * P].rearrange("(r l) -> r l", l=P)).then_inc(done, 16)
                sp.dma_start(wr[RF:RF + 1, CF, 0:REST],
                             weight[FULL * P:E].rearrange("(r l) -> r l", r=1)).then_inc(done, 16)

            sp.wait_ge(zeroed, 1)
            load_edges(src, dst, edge_weight.bitcast(i32), ints_in)
            sp.wait_ge(flag_ok, 1)
            unsorted = sp.value_load(flags[0:1, 0:1])
            with sp.If(unsorted > 0):
                with sp.Fori(0, E // CW) as c:
                    sp.wait_ge(chunk_free, c + 1)
                    sp.dma_start(chunk[:, :], dst[ds(c * CW, CW)].rearrange("(a e) -> a e", a=1)
                                 .broadcast_to([P, CW])).then_inc(chunk_in, 16)
                sp.wait_ge(moved_out, 16 * 3 * CH * P)
                load_edges(*(t.rearrange("e a -> (e a)") for t in (src_d, dst_d, w_d)), sorted_in)

            def node_load(i, u):
                k, step, turn = u % RING, LONG * i + u, 2 * i + u // RING
                first = step * NB
                if isinstance(i, int):
                    first = min(first, N - NB)
                if not isinstance(i, int) or turn > 0:
                    sp.wait_ge(added, 3 * (step - RING) + 2)
                sp.dma_start(xn[:, k], x[ds(first, NB), :].rearrange("(p g) d -> p g d", p=P)
                             ).then_inc(xn_in[k], 16)

            def aux_load(i, u):
                k, step, turn = u % RING, LONG * i + u, 2 * i + u // RING
                if not isinstance(i, int) or turn > 0:
                    sp.wait_ge(agg_ok, step - RING + 1)
                sp.dma_start(mk[:, k], mask_d[ds(step * EB, EB)].rearrange("(a e) -> a e", a=1)
                             .broadcast_to([P, EB])).then_inc(aux_in[k], 16)
                sp.dma_start(w9[0:9, k], wpart_d[:, ds(step * EB, EB)]).then_inc(aux_in[k], 16)

            def stores(i, u):
                k, step = u % RING, LONG * i + u
                sp.wait_ge(norm_ok, 3 * step + 3)
                p0 = (step * NB - (N - NB)) // (2 * G) if isinstance(i, int) and (step + 1) * NB > N else 0
                sp.dma_start(out[ds(step * NB, NB - p0 * 2 * G), :].rearrange("(p g) d -> p g d", g=2 * G),
                             on[p0:P, k]).then_inc(on_out[k], 16)
                sp.dma_start(last_d[ds(step, 1)].rearrange("a p f -> (a p) f"),
                             oe[:, u].rearrange("p g d -> p (g d)")).then_inc(oe_out[u], 16)

            assert (STEPS * NB - N) % (2 * G) == 0
            node_load(0, 0)
            node_load(0, 1)
            sp.wait_ge(scratch_out, 16 * 10)
            aux_load(0, 0)
            aux_load(0, 1)

            def step_of(i, u):
                j, v = i + (u + 2) // LONG, (u + 2) % LONG
                if not isinstance(i, int) or LONG * j + v < STEPS:
                    node_load(j, v)
                    aux_load(j, v)
                stores(i, u)

            for u in range(LONG):
                step_of(0, u)
            with sp.Fori(1, ROUNDS - 1) as i:
                for u in range(LONG):
                    step_of(i, u)
            for u in range(LONG):
                step_of(ROUNDS - 1, u)
            for u in range(LEFT):
                step_of(ROUNDS, u)
            for j in range(LONG):
                sp.wait_ge(oe_out[j], 16 * (ROUNDS + (j < LEFT)))
                sp.wait_ge(scattered[j], 16 * G * (ROUNDS + (j < LEFT)))

            def row_load(i, u):
                if not isinstance(i, int) or i > 0:
                    sp.wait_ge(late_out[u], 16 * G * i)
                sp.dma_start(rs[:, u].rearrange("p g d -> p (g d)"),
                             last_d[ds(RING * i + u, 1)].rearrange("a p f -> (a p) f")).then_inc(rs_in[u], 16)

            sp.wait_ge(flag_ok, 2)
            late = sp.value_load(flags[0:1, 1:2])
            with sp.If(late > 0):
                for u in range(RING):
                    row_load(0, u)
                with sp.Fori(1, STEPS // RING) as i:
                    for u in range(RING):
                        row_load(i, u)
                for u in range(STEPS % RING):
                    row_load(STEPS // RING, u)
                for j in range(RING):
                    sp.wait_ge(late_out[j], 16 * G * (STEPS // RING + (j < STEPS % RING)))

        @block.gpsimd
        def _(pool):
            pool.memset(ident[:, :], 0.0).then_inc(ident_ok, 1)
            pool.wait_ge(ident_ok, 1)
            pool.affine_select(out=ident[:, :], in_=ident[:, :], compare_op=ALU.not_equal, fill=1.0, base=0,
                               pattern=[[-1, P]], channel_multiplier=1).then_inc(ident_ok, 1)

            for c in range(CH):
                pool.iota(limit[:, c * P:(c + 1) * P], pattern=[[0, P]],
                          base=(c * P + 1) * (NB // G) + AHEAD * NB, channel_multiplier=NB // G)
                pool.iota(place_i[:, c * P:(c + 1) * P], pattern=[[1, P]], base=c * P * P, channel_multiplier=P)
            pool.iota(chunk[:, :], pattern=[[1, CW]], base=0, channel_multiplier=0).then_inc(iota_ok, 1)

            pool.wait_ge(flag_ok, 1)
            unsorted = pool.value_load(flags[0:1, 0:1])
            with pool.If(unsorted > 0):
                pool.sem_inc(moved_free, 1)
                with pool.Fori(0, CH * P) as c:
                    pool.wait_ge(moved_ok, c + 1)
                    pool.nop(nofuse=True)
                    for k, t in ((1, src_d), (2, dst_d), (3, w_d)):
                        pool.indirect_dma_start(t[:, :], bass.IndirectOffsetOnAxis(ap=moved[:, 0:1], axis=0),
                                                moved[:, k:k + 1], None, bounds_check=E - 1, oob_is_err=False
                                                ).then_inc(moved_out, 16)
                    pool.wait_ge(moved_out, (c + 1) * 48)
                    pool.nop(nofuse=True)
                    pool.sem_inc(moved_free, 1)

            def gathers(i, u):
                k, step, turn = u % RING, LONG * i + u, 2 * i + u // RING
                reused = not isinstance(i, int) or turn > 0
                pool.wait_ge(gi_ok, step + 1)
                if reused:
                    pool.wait_ge(e_xT, step - RING + 1)
                pool.nop(nofuse=True)
                for j in range(G):
                    pool.indirect_dma_start(xs[:, k, j, :], None, x[:, :],
                                            bass.IndirectOffsetOnAxis(ap=gi[:, k, 0, j:j + 1], axis=0)
                                            ).then_inc(gathered[k], 16)
                if reused:
                    pool.wait_ge(added, 3 * (step - RING) + 3)
                    pool.nop(nofuse=True)
                for j in range(G):
                    pool.indirect_dma_start(xd[:, k, j, :], None, x[:, :],
                                            bass.IndirectOffsetOnAxis(ap=gi[:, k, 1, j:j + 1], axis=0)
                                            ).then_inc(gathered[k], 16)

            def scatters(i, u):
                step = LONG * i + u
                pool.wait_ge(si_ok, step + 1)
                pool.wait_ge(norm_ok, 3 * step + 3)
                if not isinstance(i, int) or step + AHEAD < STEPS:
                    pool.wait_ge(on_out[(u + AHEAD) % RING], 16 * (2 * i + (u + AHEAD) // RING + 1))
                pool.nop(nofuse=True)
                for j in range(G):
                    pool.indirect_dma_start(out[:, :], bass.IndirectOffsetOnAxis(ap=si[:, u, j:j + 1], axis=0),
                                            oe[:, u, j, :], None, bounds_check=N - 1, oob_is_err=False
                                            ).then_inc(scattered[u], 16)

            for u in range(LAG):
                gathers(0, u)
            for j in range(AHEAD):
                pool.wait_ge(on_out[j], 16)
            gathers(0, LAG)
            scatters(0, 0)
            with pool.Fori(1, ROUNDS) as i:
                for u in range(LONG):
                    gathers(i, u)
                    scatters(i - (u < LAG), (u - LAG) % LONG)
            for u in range(LEFT):
                gathers(ROUNDS, u)
                scatters(ROUNDS - 1, (u - LAG) % LONG)
            for step in range(STEPS - LAG, STEPS):
                scatters(step // LONG, step % LONG)
            for j in range(LONG):
                pool.wait_ge(scattered[j], 16 * G * (ROUNDS + (j < LEFT)))

            def late_scatters(i, u):
                pool.wait_ge(li_ok, RING * i + u + 1)
                pool.wait_ge(rs_in[u], 16 * (i + 1))
                pool.nop(nofuse=True)
                for j in range(G):
                    pool.indirect_dma_start(out[:, :], bass.IndirectOffsetOnAxis(ap=li[:, u, j:j + 1], axis=0),
                                            rs[:, u, j, :], None, bounds_check=N - 1, oob_is_err=False
                                            ).then_inc(late_out[u], 16)

            pool.wait_ge(flag_ok, 2)
            late = pool.value_load(flags[0:1, 1:2])
            with pool.If(late > 0):
                with pool.Fori(0, STEPS // RING) as i:
                    for u in range(RING):
                        late_scatters(i, u)
                for u in range(STEPS % RING):
                    late_scatters(STEPS // RING, u)
                for j in range(RING):
                    pool.wait_ge(late_out[j], 16 * G * (STEPS // RING + (j < STEPS % RING)))

        @block.tensor
        def _(pe):
            pe.wait_ge(weights_in, 16 * NW)
            nc.tensor.matmul(pZe[:, 0:1], u1b[:, :], b2c[:, :], start=True, stop=True).then_inc(b2u_done, 1)
            for k in range(2):
                pe.wait_ge(flag_in, k + 1)
                nc.tensor.matmul(pHn[0:1, k:k + 1], flagp[:, k:k + 1], ones1[:, :], start=True, stop=True
                                 ).then_inc(flag_sum, 1)
            pe.wait_ge(ident_ok, 2)
            pe.wait_ge(indices_ok, 1)
            for bk, t in ((pXs, srcf), (pXdH, dstf), (pMU, nowf), (pXn, latef)):
                for c in range(CH):
                    nc.tensor.transpose(bk[:, c * P:(c + 1) * P], t[:, c * P:(c + 1) * P], ident[:, :]
                                        ).then_inc(tables_T, 1)
            pe.wait_ge(zeroed, 1)
            pe.wait_ge(tables_ok, 4)
            pe.wait_ge(flag_ok, 2)

            def transpose_edges(i, u):
                pe.wait_ge(gathered[u], 16 * 2 * G * (i + 1))
                for bk, t in ((pXs, xs), (pXdH, xd)):
                    for j in range(G):
                        last = nc.tensor.transpose(bk[:, j * P:(j + 1) * P], t[:, u, j, :], ident[:, :])
                last.then_inc(e_xT, 1)

            def transpose_nodes(i, u, b):
                if b == 0:
                    pe.wait_ge(xn_in[u], 16 * (i + 1))
                else:
                    pe.wait_ge(xnT_ok, 2 * (RING * i + u) + 1)
                for j in range(G):
                    last = nc.tensor.transpose(pXn[:, j * P:(j + 1) * P], xn[:, u, b * G + j, :], ident[:, :])
                last.then_inc(n_xT, 1)

            def message_hidden(i, u):
                step = RING * i + u
                pe.wait_ge(aux_in[u], 32 * (i + 1))
                pe.wait_ge(xsT_ok, step + 1)
                pe.wait_ge(xdT_ok, step + 1)
                nc.tensor.matmul(pXdH[:, :], wc9[:, :], w9[:, u, :], start=True, stop=False)
                nc.tensor.matmul(pXdH[:, :], w1a[:, :], xsT[:, :], start=False, stop=False)
                nc.tensor.matmul(pXdH[:, :], w1b[:, :], xdT[:, :], start=False, stop=True).then_inc(e_h1, 1)

            def messages(i, u):
                pe.wait_ge(h1_ok, RING * i + u + 1)
                nc.tensor.matmul(pMU[:, :], w2[:, :], h1[:, :], start=True, stop=True).then_inc(e_msg, 1)

            def update_hidden(i, u):
                pe.wait_ge(agg_ok, RING * i + u + 1)
                nc.tensor.matmul(pMU[:, :], u1a[:, :], xdT[:, :], start=True, stop=False)
                nc.tensor.matmul(pMU[:, :], u1b[:, :], agg[:, u % 2, :], start=False, stop=True).then_inc(e_h2, 1)

            def updates(bk, hT, done):
                nc.tensor.matmul(bk[:, :], ones[:, :], c23[:, :], start=True, stop=False)
                for j in range(G):
                    last = nc.tensor.matmul(bk[:, j * P:(j + 1) * P], hT[:, j * P:(j + 1) * P], u2[:, :],
                                            start=False, stop=(j == G - 1))
                last.then_inc(done, 1)

            def node_hidden(i, u, b):
                pe.wait_ge(xnT_ok, 2 * (RING * i + u) + b + 1)
                nc.tensor.matmul(pHn[:, :], u1a[:, :], xnT[:, b, :], start=True, stop=True).then_inc(n_h, 1)

            def node_updates(i, u, b, first):
                step = RING * i + u
                pe.wait_ge(hn_ok, 2 * step + b + 1)
                if not first:
                    pe.wait_ge(added, 3 * (step - 1) + b + 1)
                updates(pZn[b], hn[:, b, :], n_z)

            def edge_updates(i, u, first):
                step = RING * i + u
                pe.wait_ge(h2_ok, step + 1)
                if not first:
                    pe.wait_ge(added, 3 * (step - 1) + 3)
                updates(pZe, h2[:, :], e_z)

            def step_of(i, u, first=False, last=False):
                j, v = i + (u + 1) // RING, (u + 1) % RING
                message_hidden(i, u)
                transpose_nodes(i, u, 1)
                node_hidden(i, u, 0)
                messages(i, u)
                node_updates(i, u, 0, first)
                node_hidden(i, u, 1)
                update_hidden(i, u)
                node_updates(i, u, 1, first)
                if not last:
                    transpose_edges(j, v)
                    transpose_nodes(j, v, 0)
                edge_updates(i, u, first)

            pe.wait_ge(c1e_ok, 1)
            pe.wait_ge(parts_in, 16 * 12)
            transpose_edges(0, 0)
            transpose_nodes(0, 0, 0)
            for u in range(RING):
                step_of(0, u, first=(u == 0))
            with pe.Fori(1, PE_ROUNDS) as i:
                for u in range(RING):
                    step_of(i, u)
            for u in range(LEFT):
                step_of(PE_ROUNDS, u, last=(u == LEFT - 1))

        @block.scalar
        def _(act):
            act.dma_start(row2[0:1, 0, :], W1[2 * D:2 * D + 1, :]).then_inc(rows_in, 16)
            act.dma_start(row2[0:1, 1, :], c2.rearrange("(a d) -> a d", a=1)).then_inc(rows_in, 16)
            for t, a in ((w1a, W1[0:D, :]), (w1b, W1[D:2 * D, :]), (w2, W2[:, :]), (u1a, U1[0:D, :]),
                         (u1b, U1[D:2 * D, :]), (u2, U2[:, :])):
                act.dma_start(t[:, :], a).then_inc(weights_in, 16)
            for t, a in ((b1c, b1), (b2c, b2), (c1c, c1)):
                act.dma_start(t[:, :], a.rearrange("(d a) -> d a", a=1)).then_inc(weights_in, 16)
            act.dma_start(c1e[:, :], c1.rearrange("(d a) -> d a", a=1)).then_inc(weights_in, 16)
            act.wait_ge(parts_ok, 1)
            for c in range(3):
                for a in range(3):
                    act.dma_start(wc9[3 * c + a:3 * c + a + 1, :], part2[0:1, c, 0, :]).then_inc(parts_in, 16)
                act.dma_start(c23[c:c + 1, :], c2rep[0:1, c].rearrange("p g d -> p (g d)")).then_inc(parts_in, 16)
            act.wait_ge(scratch_ok, 1)
            cr = "(c r l) -> r c l"
            act.dma_start(mask_d.rearrange(cr, r=P, l=P), maskr[:, :, :]).then_inc(scratch_out, 16)
            for c in range(3):
                for a in range(3):
                    act.dma_start(wpart_d[3 * c + a].rearrange(cr, r=P, l=P), wp[:, a]).then_inc(scratch_out, 16)

            def gather_rows(i, u):
                k, turn = u % RING, 2 * i + u // RING
                if not isinstance(i, int) or turn > 0:
                    act.wait_ge(gathered[k], 16 * 2 * G * turn)
                col = (LONG * i + u) * G
                nc.scalar.copy(gi[:, k, 0, :], src_t[:, ds(col, G)])
                nc.scalar.copy(gi[:, k, 1, :], dst_t[:, ds(col, G)]).then_inc(gi_ok, 1)

            def scatter_rows(i, u):
                if not isinstance(i, int) or i > 0:
                    act.wait_ge(scattered[u], 16 * G * i)
                nc.scalar.copy(si[:, u, :], now_t[:, ds((LONG * i + u) * G, G)]).then_inc(si_ok, 1)

            act.wait_ge(tables_ok, 4)
            for u in range(RING):
                gather_rows(0, u)
            act.wait_ge(c1e_ok, 1)
            act.wait_ge(weights_in, 16 * NW)

            def edge_rows_T(i, u):
                step = LONG * i + u
                act.wait_ge(e_xT, step + 1)
                nc.scalar.copy(xsT[:, :], pXs[:, :]).then_inc(xsT_ok, 1)
                nc.scalar.copy(xdT[:, :], pXdH[:, :]).then_inc(xdT_ok, 1)

            def node_rows_T(i, u, b):
                act.wait_ge(n_xT, 2 * (LONG * i + u) + b + 1)
                nc.scalar.copy(xnT[:, b, :], pXn[:, :]).then_inc(xnT_ok, 1)

            def node_relu(i, u, b):
                act.wait_ge(n_h, 2 * (LONG * i + u) + b + 1)
                nc.scalar.activation(hn[:, b, :], pHn[:, :], ACT.Relu, bias=c1c[:, :]).then_inc(hn_ok, 1)

            def root(i, u, b):
                act.wait_ge(var_ok, 3 * (LONG * i + u) + b + 1)
                nc.scalar.activation(std[:, b, :], mv[:, b, :, 1], ACT.Sqrt, bias=eps[:, :]).then_inc(std_ok, 1)

            def step_of(i, u, last=False):
                step = LONG * i + u
                j, v = i + (u + 1) // LONG, (u + 1) % LONG
                act.wait_ge(e_h1, step + 1)
                nc.scalar.activation(h1[:, :], pXdH[:, :], ACT.Relu, bias=b1c[:, :]).then_inc(h1_ok, 1)
                node_rows_T(i, u, 1)
                node_relu(i, u, 0)
                node_relu(i, u, 1)
                root(i, u, 0)
                act.wait_ge(e_h2, step + 1)
                nc.scalar.activation(h2[:, :], pMU[:, :], ACT.Relu, bias=c1e[:, :]).then_inc(h2_ok, 1)
                if not last:
                    edge_rows_T(j, v)
                    node_rows_T(j, v, 0)
                scatter_rows(i, u)
                if not isinstance(i, int) or LONG * i + u + RING < STEPS:
                    gather_rows(i + (u + RING) // LONG, (u + RING) % LONG)
                root(i, u, 1)
                root(i, u, 2)

            edge_rows_T(0, 0)
            node_rows_T(0, 0, 0)
            for u in range(LONG):
                step_of(0, u)
            with act.Fori(1, ROUNDS - 1) as i:
                for u in range(LONG):
                    step_of(i, u)
            for u in range(LONG):
                step_of(ROUNDS - 1, u)
            for u in range(LEFT):
                step_of(ROUNDS, u, last=(u == LEFT - 1))

            def late_rows(i, u):
                if not isinstance(i, int) or i > 0:
                    act.wait_ge(late_out[u], 16 * G * i)
                nc.scalar.copy(li[:, u, :], late_t[:, ds((RING * i + u) * G, G)]).then_inc(li_ok, 1)

            act.wait_ge(flag_ok, 2)
            late = act.value_load(flags[0:1, 1:2])
            with act.If(late > 0):
                for u in range(RING):
                    late_rows(0, u)
                with act.Fori(1, STEPS // RING) as i:
                    for u in range(RING):
                        late_rows(i, u)
                for u in range(STEPS % RING):
                    late_rows(STEPS // RING, u)

        @block.vector
        def _(dve):
            links = [0]

            def link(ins):
                links[0] += 1
                ins.then_inc(chain, 1)
                dve.wait_ge(chain, links[0])

            sort_links = [0]

            def sort_link(ins):
                sort_links[0] += 1
                ins.then_inc(sort_chain, 1)
                dve.wait_ge(sort_chain, sort_links[0])

            nc.vector.memset(ints[:, 0], 0)
            nc.vector.memset(ints[:, 1:4], -1)
            nc.vector.memset(wrow[:, :, :], 0.0)
            nc.vector.memset(wc9[:, :], 0.0)
            nc.vector.memset(c23[:, :], 0.0)
            nc.vector.memset(w9[:, :, :], 0.0)
            nc.vector.memset(eps[:, :], EPS)
            nc.vector.memset(ones1[:, :], 1.0)
            nc.vector.memset(rank[:, :], 0.0)
            nc.vector.memset(ones[:, :], 1.0).then_inc(zeroed, 1)
            dve.wait_ge(zeroed, 1)

            def three_parts(part, rest):
                for a in range(3):
                    link(nc.vector.tensor_copy(part[:, a], rest))
                    if a < 2:
                        link(nc.vector.tensor_tensor(rest, rest, part[:, a], ALU.subtract))

            dve.wait_ge(ints_in, 16 * 17)
            flat = [ints[:, k].rearrange("r c l -> r (c l)") for k in range(4)]
            wflat = wrow[:, :, :].rearrange("r c l -> r (c l)")

            def flag(k, which):
                link(nc.vector.tensor_reduce(flagp[:, k:k + 1], which, mybir.AxisListType.X, ALU.max))
                dve.nop(nofuse=True)
                dve.sem_inc(flag_in, 1)
                dve.wait_ge(flag_sum, k + 1)
                nc.vector.tensor_copy(flags[0:1, k:k + 1], pHn[0:1, k:k + 1]).then_inc(flag_ok, 1)
                dve.wait_ge(flag_ok, k + 1)

            link(nc.vector.tensor_tensor(lastf[:, :], flat[1], flat[2], ALU.is_lt))
            flag(0, lastf[:, :])
            dve.wait_ge(iota_ok, 1)

            unsorted = dve.value_load(flags[0:1, 0:1])
            with dve.If(unsorted > 0):
                UNIT = 2.0 ** -16
                sort_link(nc.vector.tensor_copy(dstf[:, :], flat[1]))
                nc.vector.tensor_scalar(place[:, :], place_i[:, :], UNIT, None, ALU.mult)
                sort_link(nc.vector.tensor_scalar(chunk_pos[:, :], chunk[:, :], UNIT, None, ALU.mult))
                dve.nop(nofuse=True)
                dve.sem_inc(chunk_free, 1)
                with dve.Fori(0, E // CW) as c:
                    dve.wait_ge(chunk_in, 16 * (c + 1))
                    dve.nop(nofuse=True)
                    dve.sem_inc(counted, 1)
                    with dve.Fori(0, CH * P) as m:
                        dve.wait_ge(counted, c * (CH * P + 2) + m + 1)
                        nc.vector.scalar_tensor_tensor(out=before[:, :], in0=chunk[:, :],
                                                       scalar=dstf[:, ds(m, 1)], in1=chunk_pos[:, :],
                                                       op0=ALU.subtract, op1=ALU.add).then_inc(compared, 1)
                        dve.wait_ge(compared, c * (CH * P) + m + 1)
                        nc.vector.tensor_scalar(before[:, :], before[:, :], place[:, ds(m, 1)], None, ALU.is_lt,
                                                ALU.add, accum_out=count[:, ds(m, 1)]).then_inc(counted, 1)
                    dve.wait_ge(counted, (c + 1) * (CH * P + 2) - 1)
                    nc.vector.tensor_tensor(rank[:, :], rank[:, :], count[:, :], ALU.add)
                    nc.vector.tensor_scalar(place[:, :], place[:, :], -CW * UNIT, None, ALU.add).then_inc(counted, 1)
                    dve.wait_ge(counted, (c + 1) * (CH * P + 2))
                    dve.nop(nofuse=True)
                    dve.sem_inc(chunk_free, 1)
                sort_link(nc.vector.tensor_scalar(lastf[:, :], flat[1], 0.0, None, ALU.is_ge))
                sort_link(nc.vector.scalar_tensor_tensor(out=rank[:, :], in0=rank[:, :], scalar=float(-SKIP),
                                                         in1=lastf[:, :], op0=ALU.add, op1=ALU.mult))
                sort_link(nc.vector.tensor_scalar(rank[:, :], rank[:, :], float(SKIP), None, ALU.add))
                with dve.Fori(0, CH * P) as m:
                    dve.wait_ge(moved_free, m + 1)
                    nc.vector.tensor_copy(moved[:, 0:1], rank[:, ds(m, 1)])
                    nc.vector.tensor_copy(moved[:, 1:2], flat[0][:, ds(m, 1)])
                    nc.vector.tensor_copy(moved[:, 2:3], flat[1][:, ds(m, 1)])
                    nc.vector.tensor_copy(moved[:, 3:4].bitcast(f32), wflat[:, ds(m, 1)]).then_inc(moved_ok, 1)
                dve.wait_ge(sorted_in, 16 * 17)
                dve.nop(nofuse=True)

            nc.vector.tensor_copy(srcf[:, :], flat[0])
            nc.vector.tensor_scalar(dstf[:, :], flat[1], 0.0, None, ALU.max)
            nc.vector.tensor_tensor(lastf[:, :], flat[1], flat[3], ALU.not_equal)
            link(nc.vector.tensor_tensor(latef[:, :], flat[1], limit[:, :], ALU.is_ge))
            link(nc.vector.tensor_tensor(latef[:, :], latef[:, :], lastf[:, :], ALU.mult))
            nc.vector.tensor_tensor(nowf[:, :], lastf[:, :], latef[:, :], ALU.subtract)
            flag(1, latef[:, :])
            for t in (nowf, latef):
                link(nc.vector.scalar_tensor_tensor(out=t[:, :], in0=flat[1], scalar=float(-SKIP), in1=t[:, :],
                                                    op0=ALU.add, op1=ALU.mult))
                link(nc.vector.tensor_scalar(t[:, :], t[:, :], float(SKIP), None, ALU.add))
            dve.nop(nofuse=True)
            dve.sem_inc(indices_ok, 1)
            link(nc.vector.tensor_tensor(lastf[:, :], flat[1], flat[2], ALU.not_equal))
            link(nc.vector.tensor_scalar(maskr[:, :, :].rearrange("r c l -> r (c l)"), lastf[:, :], NEG, None,
                                         ALU.mult))
            three_parts(wp, wrow[:, :, :])
            dve.wait_ge(chain, links[0])
            dve.nop(nofuse=True)
            dve.sem_inc(scratch_ok, 1)
            dve.wait_ge(rows_in, 32)
            three_parts(part2, row2[:, :, :])
            for g in range(G):
                last = nc.vector.tensor_copy(c2rep[:, :, g, :], part2[:, :, 1, :])
            last.then_inc(parts_ok, 1)
            for n, (t, bk) in enumerate(((src_t, pXs), (dst_t, pXdH), (now_t, pMU), (late_t, pXn))):
                dve.wait_ge(tables_T, CH * (n + 1))
                nc.vector.tensor_copy(t[:, :], bk[:, 0:CH * P]).then_inc(tables_ok, 1)
            dve.wait_ge(b2u_done, 1)
            dve.wait_ge(weights_in, 16 * NW)
            nc.vector.tensor_tensor(c1e[:, :], c1e[:, :], pZe[:, 0:1], ALU.add).then_inc(c1e_ok, 1)

            def running_max(i, u, first=False):
                step = LONG * i + u
                dve.wait_ge(e_msg, step + 1)
                if not first:
                    dve.wait_ge(agg_ok, step)
                nc.vector.tensor_tensor_scan(agg[:, u % 2, :], mk[:, u % RING, :], pMU[:, :],
                                             NEG if first else agg[:, (u + 1) % 2, EB - 1:EB],
                                             ALU.add, ALU.max).then_inc(agg_ok, 1)

            def result(u, b):
                k = u % RING
                if b < 2:
                    return on[:, k, b * G:(b + 1) * G, :], pZn[b], xn[:, k, b * G:(b + 1) * G, :]
                return oe[:, u], pZe, xd[:, k]

            def residual(i, u, b):
                z, bk, rows = result(u, b)
                batch = 3 * (LONG * i + u) + b
                if b < 2:
                    dve.wait_ge(n_z, 2 * (LONG * i + u) + b + 1)
                else:
                    dve.wait_ge(e_z, LONG * i + u + 1)
                turn = 2 * i + u // RING
                if b == 0 and (not isinstance(i, int) or turn > 0):
                    dve.wait_ge(on_out[u % RING], 16 * turn)
                if b == 2 and (not isinstance(i, int) or i > 0):
                    dve.wait_ge(oe_out[u], 16 * i)
                    dve.wait_ge(scattered[u], 16 * G * i)
                nc.vector.tensor_tensor(z, bk[:, :].rearrange("p (g d) -> p g d", g=G), rows, ALU.add
                                        ).then_inc(added, 1)
                dve.wait_ge(added, batch + 1)
                for g in range(G):
                    last = nc.vector.bn_stats(stats[:, b, g, :], z[:, g, :])
                last.then_inc(stat_ok, 1)
                dve.wait_ge(stat_ok, batch + 1)
                dve.nop(nofuse=True)
                for g in range(G):
                    last = nc.vector.bn_aggr(mv[:, b, g, :], stats[:, b, g, :])
                last.then_inc(var_ok, 1)

            def normalise(i, u, b):
                z, _, _ = result(u, b)
                batch = 3 * (LONG * i + u) + b
                dve.wait_ge(std_ok, batch + 1)
                nc.vector.reciprocal(rstd[:, b, :], std[:, b, :]).then_inc(rstd_ok, 1)
                dve.wait_ge(rstd_ok, batch + 1)
                for g in range(G):
                    last = nc.vector.tensor_scalar(z[:, g, :], z[:, g, :], mv[:, b, g, 0:1], rstd[:, b, g:g + 1],
                                                   ALU.subtract, ALU.mult)
                last.then_inc(norm_ok, 1)

            def step_of(i, u, first=False):
                running_max(i, u, first)
                residual(i, u, 0)
                residual(i, u, 1)
                normalise(i, u, 0)
                residual(i, u, 2)
                normalise(i, u, 1)
                normalise(i, u, 2)

            for u in range(LONG):
                step_of(0, u, first=(u == 0))
            with dve.Fori(1, ROUNDS) as i:
                for u in range(LONG):
                    step_of(i, u)
            for u in range(LEFT):
                step_of(ROUNDS, u)


_INS = ['x', 'src', 'dst', 'edge_weight', 'L0_gnn_W1', 'L0_gnn_b1', 'L0_gnn_W2', 'L0_gnn_b2',
        'L0_gnn_U1', 'L0_gnn_c1', 'L0_gnn_U2', 'L0_gnn_c2']


def kernel(**inputs):
    import concourse.bacc as _bacc
    from concourse.bass_utils import run_bass_kernel_spmd as _run

    nc = _bacc.Bacc("TRN2", target_bir_lowering=False, num_devices=1)
    arrays, args = {}, []
    for name in _INS:
        a = np.ascontiguousarray(inputs[name])
        arrays[f"in_{name}_dram"] = a
        args.append(nc.dram_tensor(f"in_{name}_dram", a.shape, mybir.dt.from_np(a.dtype), kind="ExternalInput").ap())
    x = inputs['x']
    args.append(nc.dram_tensor("out_0_dram", x.shape, mybir.dt.float32, kind="ExternalOutput").ap())
    build(nc, *args)
    r = _run(nc, [arrays], core_ids=[0])
    return r.results[0]["out_0_dram"]
```

```python
import numpy as np
import concourse.bass as bass
from concourse import mybir
from contextlib import ExitStack

P = 128


def build(nc, x, src, dst, edge_weight, W1, b1, W2, b2, U1, c1, U2, c2, out):
    f32, bf16, i32 = mybir.dt.float32, mybir.dt.bfloat16, mybir.dt.int32
    ALU, ACT = mybir.AluOpType, mybir.ActivationFunctionType
    ds = bass.ds

    N, D = x.shape
    E = src.shape[0]
    assert D == P
    EB = 512
    G = EB // P
    STEPS = -(-E // EB)
    NB = 2 * EB
    assert -(-N // NB) == STEPS
    RING = 4
    LONG = 8
    LAG = LONG - 2
    AHEAD = 1
    LEFT = STEPS % LONG
    ROUNDS = STEPS // LONG
    PE_ROUNDS = STEPS // RING
    assert LONG == 2 * RING and 1 <= LEFT < RING
    CH = -(-E // (P * P))
    EP = CH * P * P
    FULL = E // P
    REST = E - FULL * P
    CF = FULL // P
    RF = FULL - CF * P
    SKIP = 1 << 20
    NEG = -3.0e38
    EPS = 1e-5

    with ExitStack() as ctx:
        def sb(name, shape, dt=f32):
            return ctx.enter_context(nc.sbuf_tensor(name, shape, dt))

        def sem(name):
            return ctx.enter_context(nc.semaphore(name))

        mask_d = nc.dram_tensor("mask_d", (EP + 1,), bf16).ap()
        wpart_d = nc.dram_tensor("wpart_d", (CH * P, 3, 3, P), bf16).ap()
        part_d = nc.dram_tensor("part_d", (3, 2, D), bf16).ap()
        src_d, dst_d = (nc.dram_tensor(n, (E, 1), i32).ap() for n in ("src_d", "dst_d"))
        w_d = nc.dram_tensor("w_d", (E, 1), i32).ap()
        last_d = nc.dram_tensor("last_d", (STEPS, P, G * D), f32).ap()

        w1a, w1b, w2 = sb("w1a", [P, D]), sb("w1b", [P, D]), sb("w2", [P, D])
        u1a, u1b, u2 = sb("u1a", [P, D]), sb("u1b", [P, D]), sb("u2", [P, D])
        b1c, b2c, c1c, c1e, eps = (sb(n, [P, 1]) for n in ("b1c", "b2c", "c1c", "c1e", "eps"))
        eps2 = sb("eps2", [P, 1])
        mask0 = sb("mask0", [1, 1], bf16)
        ident = sb("ident", [P, P])
        row2 = sb("row2", [1, 2, D])
        part2 = sb("part2", [1, 3, 2, D], bf16)
        wc9 = sb("wc9", [P, D], bf16)
        c23 = sb("c23", [P, G * D], bf16)
        ones = sb("ones", [P, P], bf16)

        ints = sb("ints", [P, 3, CH, P], i32)
        wrow = sb("wrow", [P, CH, P])
        srcf, dstf, lastf, nowf, latef = (sb(n, [P, CH * P]) for n in ("srcf", "dstf", "lastf", "nowf", "latef"))
        limit = sb("limit", [P, CH * P], i32)
        flagp = sb("flagp", [P, 2])
        ones1 = sb("ones1", [P, 1])
        flags = sb("flags", [1, 2], i32)
        maskr = sb("maskr", [P, CH, P], bf16)
        wp = sb("wp", [P, CH, 3, P], bf16)
        src_t, dst_t, now_t, late_t = (sb(n, [P, CH * P], i32) for n in ("src_t", "dst_t", "now_t", "late_t"))

        CW = E // 16
        assert CW * 16 == E
        chunk = sb("chunk", [P, CW], i32)
        chunk_pos = sb("chunk_pos", [P, CW])
        before = sb("before", [P, CW])
        place = sb("place", [P, CH * P])
        place_i = sb("place_i", [P, CH * P], i32)
        count = sb("count", [P, CH * P])
        rank = sb("rank", [P, CH * P])
        moved = sb("moved", [P, 4], i32)

        gi = sb("gi", [P, RING, 2, G], i32)
        si = sb("si", [P, LONG, G], i32)
        li = sb("li", [P, RING, G], i32)
        xs = sb("xs", [P, RING, G, D])
        xd = sb("xd", [P, RING, G, D])
        mk = sb("mk", [P, RING, EB], bf16)
        w9 = sb("w9", [P, RING, EB], bf16)
        xn = sb("xn", [P, RING, 2 * G, D])
        on = sb("on", [P, RING, 2 * G, D])
        oe = sb("oe", [P, LONG, G, D])
        rs = sb("rs", [P, RING, G, D])

        xsT, xdT, h1, h2 = (sb(n, [P, EB]) for n in ("xsT", "xdT", "h1", "h2"))
        agg = sb("agg", [P, 2, EB])
        xnT = sb("xnT", [P, 2, EB])
        hn = sb("hn", [P, 2, EB])
        stats = sb("stats", [P, 3, G, 6])
        mv = sb("mv", [P, 3, G, 2])
        std = sb("std", [P, 3, G])
        rstd = sb("rstd", [P, 3, G])

        def bank(name):
            return ctx.enter_context(nc.psum_tensor(name, [P, EB], f32))

        pXs = bank("pXs")
        pXdH = bank("pXdH")
        pMU = bank("pMU")
        pZe = bank("pZe")
        pXn = bank("pXn")
        pHn = bank("pHn")
        pZn = [bank("pZn0"), bank("pZn1")]

        padded = sem("padded")
        consts_ok = sem("consts_ok")
        zeroed = sem("zeroed")
        ident_ok = sem("ident_ok")
        weights_in = sem("weights_in")
        rows_in = sem("rows_in")
        dst_in = sem("dst_in")
        src_in = sem("src_in")
        edge_weight_in = sem("edge_weight_in")
        chain = sem("chain")
        sort_chain = sem("sort_chain")
        indices_ok = sem("indices_ok")
        scratch_ok = sem("scratch_ok")
        parts_ok = sem("parts_ok")
        parts_out = sem("parts_out")
        parts_in = sem("parts_in")
        scratch_out = sem("scratch_out")
        tables_T = sem("tables_T")
        b2u_done = sem("b2u_done")
        tables_ok = sem("tables_ok")
        c1e_ok = sem("c1e_ok")
        xn_in = [sem(f"xn_in{k}") for k in range(RING)]
        aux_in = [sem(f"aux_in{k}") for k in range(RING)]
        gathered = [sem(f"gathered{k}") for k in range(RING)]
        on_out = [sem(f"on_out{k}") for k in range(RING)]
        oe_out = [sem(f"oe_out{k}") for k in range(LONG)]
        gi_ok = sem("gi_ok")
        si_ok = sem("si_ok")
        li_ok = sem("li_ok")
        e_xT = sem("e_xT")
        e_h1 = sem("e_h1")
        e_msg = sem("e_msg")
        e_h2 = sem("e_h2")
        e_z = sem("e_z")
        n_xT = sem("n_xT")
        n_h = sem("n_h")
        n_z = sem("n_z")
        xsT_ok, xdT_ok = sem("xsT_ok"), sem("xdT_ok")
        h1_ok, h2_ok = sem("h1_ok"), sem("h2_ok")
        xnT_ok, hn_ok = sem("xnT_ok"), sem("hn_ok")
        agg_ok = sem("agg_ok")
        added = sem("added")
        stat_ok = sem("stat_ok")
        var_ok = sem("var_ok")
        std_ok = sem("std_ok")
        rstd_ok = sem("rstd_ok")
        norm_ok = sem("norm_ok")
        scattered = [sem(f"scattered{k}") for k in range(LONG)]
        rs_in = [sem(f"rs_in{k}") for k in range(RING)]
        late_out = [sem(f"late_out{k}") for k in range(RING)]
        iota_ok = sem("iota_ok")
        flag_in = sem("flag_in")
        flag_sum = sem("flag_sum")
        flag_ok = sem("flag_ok")
        chunk_free = sem("chunk_free")
        chunk_in = sem("chunk_in")
        compared = sem("compared")
        counted = sem("counted")
        moved_free = sem("moved_free")
        moved_ok = sem("moved_ok")
        moved_out = sem("moved_out")
        sorted_in = sem("sorted_in")

        NW = 10
        block = ctx.enter_context(nc.Block())

        @block.sync
        def _(sp):
            cr = "(c r l) -> r c l"

            def load_list(t, a, n, done):
                sp.dma_start(t[:, 0:CF, :], a[0:CF * P * P].rearrange(cr, r=P, l=P)).then_inc(done, 16)
                sp.dma_start(t[0:RF, CF, :], a[CF * P * P:FULL * P].rearrange("(r l) -> r l", l=P)).then_inc(done, 16)
                sp.dma_start(t[RF:RF + 1, CF, 0:n - FULL * P], a[FULL * P:n].rearrange("(r l) -> r l", r=1)
                             ).then_inc(done, 16)

            def load_edges(src, dst, weight, dst_done, src_done, weight_done):
                load_list(ints[:, 1], dst, E, dst_done)
                load_list(ints[:, 2], dst[1:E], E - 1, dst_done)
                load_list(ints[:, 0], src, E, src_done)
                load_list(wrow[:, :, :].bitcast(i32), weight, E, weight_done)

            sp.wait_ge(padded, 1)
            load_edges(src, dst, edge_weight.bitcast(i32), dst_in, src_in, edge_weight_in)
            sp.dma_start(row2[0:1, 0, :], W1[2 * D:2 * D + 1, :]).then_inc(rows_in, 16)
            sp.dma_start(row2[0:1, 1, :], c2.rearrange("(a d) -> a d", a=1)).then_inc(rows_in, 16)
            for t, a in ((w1a, W1[0:D, :]), (w1b, W1[D:2 * D, :]), (u1a, U1[0:D, :]), (w2, W2[:, :]),
                         (u2, U2[:, :]), (u1b, U1[D:2 * D, :])):
                sp.dma_start(t[:, :], a).then_inc(weights_in, 16)
            for t, a in ((b1c, b1), (b2c, b2), (c1c, c1), (c1e, c1)):
                sp.dma_start(t[:, :], a.rearrange("(d a) -> d a", a=1)).then_inc(weights_in, 16)

            sp.wait_ge(flag_ok, 1)
            unsorted = sp.value_load(flags[0:1, 0:1])
            with sp.If(unsorted > 0):
                with sp.Fori(0, E // CW) as c:
                    sp.wait_ge(chunk_free, c + 1)
                    sp.dma_start(chunk[:, :], dst[ds(c * CW, CW)].rearrange("(a e) -> a e", a=1)
                                 .broadcast_to([P, CW])).then_inc(chunk_in, 16)
                sp.wait_ge(moved_out, 16 * 3 * CH * P)
                load_edges(*(t.rearrange("e a -> (e a)") for t in (src_d, dst_d, w_d)),
                           sorted_in, sorted_in, sorted_in)

            def node_load(i, u):
                k, step, turn = u % RING, LONG * i + u, 2 * i + u // RING
                first = step * NB
                if isinstance(i, int):
                    first = min(first, N - NB)
                if not isinstance(i, int) or turn > 0:
                    sp.wait_ge(added, 3 * (step - RING) + 2)
                sp.dma_start(xn[:, k], x[ds(first, NB), :].rearrange("(p g) d -> p g d", p=P)
                             ).then_inc(xn_in[k], 16)

            def aux_load(i, u):
                k, step, turn = u % RING, LONG * i + u, 2 * i + u // RING
                if not isinstance(i, int) or turn > 0:
                    sp.wait_ge(agg_ok, step - RING + 1)
                sp.dma_start(mk[:, k], mask_d[ds(step * EB, EB)].rearrange("(a e) -> a e", a=1)
                             .broadcast_to([P, EB])).then_inc(aux_in[k], 16)
                sp.dma_start(w9[0:9, k].rearrange("q (t l) -> q t l", l=P),
                             wpart_d[ds(step * G, G)].rearrange("t c a l -> (c a) t l")).then_inc(aux_in[k], 16)

            def stores(i, u):
                k, step = u % RING, LONG * i + u
                sp.wait_ge(norm_ok, 3 * step + 2)
                p0 = (step * NB - (N - NB)) // (2 * G) if isinstance(i, int) and (step + 1) * NB > N else 0
                sp.dma_start(out[ds(step * NB, NB - p0 * 2 * G), :].rearrange("(p g) d -> p g d", g=2 * G),
                             on[p0:P, k]).then_inc(on_out[k], 16)
                with sp.If(late > 0):
                    sp.wait_ge(norm_ok, 3 * step + 3)
                    sp.dma_start(last_d[ds(step, 1)].rearrange("a p f -> (a p) f"),
                                 oe[:, u].rearrange("p g d -> p (g d)")).then_inc(oe_out[u], 16)
                with sp.Else():
                    sp.sem_inc(oe_out[u], 16)

            assert (STEPS * NB - N) % (2 * G) == 0
            node_load(0, 0)
            node_load(0, 1)
            sp.wait_ge(zeroed, 1)
            sp.wait_ge(parts_ok, 1)
            sp.dma_start(part_d.rearrange("(o c) k d -> o (c k d)", o=1),
                         part2[0:1].rearrange("p c k d -> p (c k d)")).then_inc(parts_out, 16)
            sp.wait_ge(parts_out, 16)
            for c in range(3):
                sp.dma_start(wc9[3 * c:3 * c + 3, :],
                             part_d[c, 0:1, :].broadcast_to([3, D])).then_inc(parts_in, 16)
            sp.dma_start(c23[0:3, :].rearrange("c (g d) -> c g d", g=G),
                         part_d[:, 1:2, :].broadcast_to([3, G, D])).then_inc(parts_in, 16)
            sp.wait_ge(scratch_out, 16 * 5)
            aux_load(0, 0)
            aux_load(0, 1)

            sp.wait_ge(flag_ok, 2)
            late = sp.value_load(flags[0:1, 1:2])

            def step_of(i, u):
                j, v = i + (u + 2) // LONG, (u + 2) % LONG
                if not isinstance(i, int) or LONG * j + v < STEPS:
                    node_load(j, v)
                    aux_load(j, v)
                stores(i, u)

            for u in range(LONG):
                step_of(0, u)
            with sp.Fori(1, ROUNDS - 1) as i:
                for u in range(LONG):
                    step_of(i, u)
            for u in range(LONG):
                step_of(ROUNDS - 1, u)
            for u in range(LEFT):
                step_of(ROUNDS, u)
            for j in range(LONG):
                sp.wait_ge(oe_out[j], 16 * (ROUNDS + (j < LEFT)))
                sp.wait_ge(scattered[j], 16 * G * (ROUNDS + (j < LEFT)))

            def row_load(i, u):
                if not isinstance(i, int) or i > 0:
                    sp.wait_ge(late_out[u], 16 * G * i)
                sp.dma_start(rs[:, u].rearrange("p g d -> p (g d)"),
                             last_d[ds(RING * i + u, 1)].rearrange("a p f -> (a p) f")).then_inc(rs_in[u], 16)

            with sp.If(late > 0):
                for u in range(RING):
                    row_load(0, u)
                with sp.Fori(1, STEPS // RING) as i:
                    for u in range(RING):
                        row_load(i, u)
                for u in range(STEPS % RING):
                    row_load(STEPS // RING, u)
                for j in range(RING):
                    sp.wait_ge(late_out[j], 16 * G * (STEPS // RING + (j < STEPS % RING)))

        @block.gpsimd
        def _(pool):
            pool.memset(ident[:, :], 0.0).then_inc(ident_ok, 1)
            pool.memset(wc9[:, :], 0.0)
            pool.memset(c23[:, :], 0.0)
            pool.memset(w9[:, :, :], 0.0).then_inc(zeroed, 1)
            pool.wait_ge(ident_ok, 1)
            pool.affine_select(out=ident[:, :], in_=ident[:, :], compare_op=ALU.not_equal, fill=1.0, base=0,
                               pattern=[[-1, P]], channel_multiplier=1).then_inc(ident_ok, 1)

            for c in range(CH):
                last = pool.iota(limit[:, c * P:(c + 1) * P], pattern=[[0, P]],
                          base=(c * P + 1) * (NB // G) + AHEAD * NB, channel_multiplier=NB // G)
            last.then_inc(iota_ok, 1)

            pool.wait_ge(flag_ok, 1)
            unsorted = pool.value_load(flags[0:1, 0:1])
            with pool.If(unsorted > 0):
                for c in range(CH):
                    pool.iota(place_i[:, c * P:(c + 1) * P], pattern=[[1, P]], base=c * P * P,
                              channel_multiplier=P)
                pool.iota(chunk[:, :], pattern=[[1, CW]], base=0, channel_multiplier=0).then_inc(iota_ok, 1)
                pool.sem_inc(moved_free, 1)
                with pool.Fori(0, CH * P) as c:
                    pool.wait_ge(moved_ok, c + 1)
                    pool.nop(nofuse=True)
                    for k, t in ((1, src_d), (2, dst_d), (3, w_d)):
                        pool.indirect_dma_start(t[:, :], bass.IndirectOffsetOnAxis(ap=moved[:, 0:1], axis=0),
                                                moved[:, k:k + 1], None, bounds_check=E - 1, oob_is_err=False
                                                ).then_inc(moved_out, 16)
                    pool.wait_ge(moved_out, (c + 1) * 48)
                    pool.nop(nofuse=True)
                    pool.sem_inc(moved_free, 1)

            def gathers(i, u):
                k, step, turn = u % RING, LONG * i + u, 2 * i + u // RING
                reused = not isinstance(i, int) or turn > 0
                pool.wait_ge(gi_ok, step + 1)
                if reused:
                    pool.wait_ge(e_xT, step - RING + 1)
                pool.nop(nofuse=True)
                for j in range(G):
                    pool.indirect_dma_start(xs[:, k, j, :], None, x[:, :],
                                            bass.IndirectOffsetOnAxis(ap=gi[:, k, 0, j:j + 1], axis=0)
                                            ).then_inc(gathered[k], 16)
                if reused:
                    pool.wait_ge(added, 3 * (step - RING) + 3)
                    pool.nop(nofuse=True)
                for j in range(G):
                    pool.indirect_dma_start(xd[:, k, j, :], None, x[:, :],
                                            bass.IndirectOffsetOnAxis(ap=gi[:, k, 1, j:j + 1], axis=0)
                                            ).then_inc(gathered[k], 16)

            def scatters(i, u):
                step = LONG * i + u
                pool.wait_ge(si_ok, step + 1)
                pool.wait_ge(norm_ok, 3 * step + 3)
                if not isinstance(i, int) or step + AHEAD < STEPS:
                    pool.wait_ge(on_out[(u + AHEAD) % RING], 16 * (2 * i + (u + AHEAD) // RING + 1))
                pool.nop(nofuse=True)
                for j in range(G):
                    pool.indirect_dma_start(out[:, :], bass.IndirectOffsetOnAxis(ap=si[:, u, j:j + 1], axis=0),
                                            oe[:, u, j, :], None, bounds_check=N - 1, oob_is_err=False
                                            ).then_inc(scattered[u], 16)

            for u in range(LAG):
                gathers(0, u)
            for j in range(AHEAD):
                pool.wait_ge(on_out[j], 16)
            for u in range(LAG, LONG):
                gathers(0, u)
                scatters(0, u - LAG)
            with pool.Fori(1, ROUNDS) as i:
                for u in range(LONG):
                    gathers(i, u)
                    scatters(i - (u < LAG), (u - LAG) % LONG)
            for u in range(LEFT):
                gathers(ROUNDS, u)
            for step in range(STEPS - LEFT - LAG, STEPS):
                scatters(step // LONG, step % LONG)
            for j in range(LONG):
                pool.wait_ge(scattered[j], 16 * G * (ROUNDS + (j < LEFT)))

            def late_scatters(i, u):
                pool.wait_ge(li_ok, RING * i + u + 1)
                pool.wait_ge(rs_in[u], 16 * (i + 1))
                pool.nop(nofuse=True)
                for j in range(G):
                    pool.indirect_dma_start(out[:, :], bass.IndirectOffsetOnAxis(ap=li[:, u, j:j + 1], axis=0),
                                            rs[:, u, j, :], None, bounds_check=N - 1, oob_is_err=False
                                            ).then_inc(late_out[u], 16)

            pool.wait_ge(flag_ok, 2)
            late = pool.value_load(flags[0:1, 1:2])
            with pool.If(late > 0):
                with pool.Fori(0, STEPS // RING) as i:
                    for u in range(RING):
                        late_scatters(i, u)
                for u in range(STEPS % RING):
                    late_scatters(STEPS // RING, u)
                for j in range(RING):
                    pool.wait_ge(late_out[j], 16 * G * (STEPS // RING + (j < STEPS % RING)))

        @block.tensor
        def _(pe):
            def flag_count(k):
                pe.wait_ge(flag_in, k + 1)
                nc.tensor.matmul(pHn[0:1, k:k + 1], flagp[:, k:k + 1], ones1[:, :], start=True, stop=True
                                 ).then_inc(flag_sum, 1)

            def turn_tables(k, pair):
                pe.wait_ge(indices_ok, k + 1)
                for bk, t in pair:
                    for c in range(CH):
                        nc.tensor.transpose(bk[:, c * P:(c + 1) * P], t[:, c * P:(c + 1) * P], ident[:, :]
                                            ).then_inc(tables_T, 1)

            pe.wait_ge(consts_ok, 1)
            flag_count(0)
            pe.wait_ge(ident_ok, 2)
            turn_tables(0, ((pXs, srcf), (pXdH, dstf)))
            flag_count(1)
            turn_tables(1, ((pMU, nowf), (pXn, latef)))
            pe.wait_ge(weights_in, 16 * NW)
            nc.tensor.matmul(pZe[:, 0:1], u1b[:, :], b2c[:, :], start=True, stop=True).then_inc(b2u_done, 1)

            def transpose_edges(i, u):
                pe.wait_ge(gathered[u], 16 * 2 * G * (i + 1))
                for bk, t in ((pXs, xs), (pXdH, xd)):
                    for j in range(G):
                        last = nc.tensor.transpose(bk[:, j * P:(j + 1) * P], t[:, u, j, :], ident[:, :])
                last.then_inc(e_xT, 1)

            def transpose_nodes(i, u, b):
                if b == 0:
                    pe.wait_ge(xn_in[u], 16 * (i + 1))
                else:
                    pe.wait_ge(xnT_ok, 2 * (RING * i + u) + 1)
                for j in range(G):
                    last = nc.tensor.transpose(pXn[:, j * P:(j + 1) * P], xn[:, u, b * G + j, :], ident[:, :])
                last.then_inc(n_xT, 1)

            def message_hidden(i, u):
                step = RING * i + u
                pe.wait_ge(aux_in[u], 32 * (i + 1))
                pe.wait_ge(xsT_ok, step + 1)
                pe.wait_ge(xdT_ok, step + 1)
                nc.tensor.matmul(pXdH[:, :], wc9[:, :], w9[:, u, :], start=True, stop=False)
                nc.tensor.matmul(pXdH[:, :], w1a[:, :], xsT[:, :], start=False, stop=False)
                nc.tensor.matmul(pXdH[:, :], w1b[:, :], xdT[:, :], start=False, stop=True).then_inc(e_h1, 1)

            def messages(i, u):
                pe.wait_ge(h1_ok, RING * i + u + 1)
                nc.tensor.matmul(pMU[:, :], w2[:, :], h1[:, :], start=True, stop=True).then_inc(e_msg, 1)

            def update_hidden(i, u):
                pe.wait_ge(agg_ok, RING * i + u + 1)
                nc.tensor.matmul(pMU[:, :], u1a[:, :], xdT[:, :], start=True, stop=False)
                nc.tensor.matmul(pMU[:, :], u1b[:, :], agg[:, u % 2, :], start=False, stop=True).then_inc(e_h2, 1)

            def updates(bk, hT, done):
                nc.tensor.matmul(bk[:, :], ones[:, :], c23[:, :], start=True, stop=False)
                for j in range(G):
                    last = nc.tensor.matmul(bk[:, j * P:(j + 1) * P], hT[:, j * P:(j + 1) * P], u2[:, :],
                                            start=False, stop=(j == G - 1))
                last.then_inc(done, 1)

            def node_hidden(i, u, b):
                pe.wait_ge(xnT_ok, 2 * (RING * i + u) + b + 1)
                nc.tensor.matmul(pHn[:, :], u1a[:, :], xnT[:, b, :], start=True, stop=True).then_inc(n_h, 1)

            def node_updates(i, u, b, first):
                step = RING * i + u
                pe.wait_ge(hn_ok, 2 * step + b + 1)
                if not first:
                    pe.wait_ge(added, 3 * (step - 1) + b + 1)
                updates(pZn[b], hn[:, b, :], n_z)

            def edge_updates(i, u, first):
                step = RING * i + u
                pe.wait_ge(h2_ok, step + 1)
                if not first:
                    pe.wait_ge(added, 3 * (step - 1) + 3)
                updates(pZe, h2[:, :], e_z)

            def step_of(i, u, first=False, last=False):
                j, v = i + (u + 1) // RING, (u + 1) % RING
                message_hidden(i, u)
                transpose_nodes(i, u, 1)
                node_hidden(i, u, 0)
                messages(i, u)
                node_updates(i, u, 0, first)
                node_hidden(i, u, 1)
                update_hidden(i, u)
                node_updates(i, u, 1, first)
                if not last:
                    transpose_edges(j, v)
                    transpose_nodes(j, v, 0)
                edge_updates(i, u, first)

            transpose_edges(0, 0)
            pe.wait_ge(tables_ok, 4)
            transpose_nodes(0, 0, 0)
            pe.wait_ge(flag_ok, 2)
            pe.wait_ge(c1e_ok, 1)
            pe.wait_ge(parts_in, 16 * 4)
            for u in range(RING):
                step_of(0, u, first=(u == 0))
            with pe.Fori(1, PE_ROUNDS) as i:
                for u in range(RING):
                    step_of(i, u)
            for u in range(LEFT):
                step_of(PE_ROUNDS, u, last=(u == LEFT - 1))

        @block.scalar
        def _(act):
            def gather_rows(i, u):
                k, turn = u % RING, 2 * i + u // RING
                if not isinstance(i, int) or turn > 0:
                    act.wait_ge(gathered[k], 16 * 2 * G * turn)
                col = (LONG * i + u) * G
                nc.scalar.copy(gi[:, k, 0, :], src_t[:, ds(col, G)])
                nc.scalar.copy(gi[:, k, 1, :], dst_t[:, ds(col, G)]).then_inc(gi_ok, 1)

            def scatter_rows(i, u):
                if not isinstance(i, int) or i > 0:
                    act.wait_ge(scattered[u], 16 * G * i)
                nc.scalar.copy(si[:, u, :], now_t[:, ds((LONG * i + u) * G, G)]).then_inc(si_ok, 1)

            act.wait_ge(consts_ok, 1)
            nc.scalar.activation(eps2[:, :], eps[:, :], ACT.Sqrt)
            act.wait_ge(tables_ok, 2)
            for u in range(RING):
                gather_rows(0, u)
            act.wait_ge(scratch_ok, 1)
            for c in range(3):
                act.dma_start(wpart_d[:, c].rearrange("(c r) a l -> r c (a l)", r=P),
                              wp[:, :, :, :].rearrange("r c a l -> r c (a l)")).then_inc(scratch_out, 16)
            act.dma_start(mask_d[1:1 + EP].rearrange("(c r l) -> r c l", r=P, l=P), maskr[:, :, :]
                          ).then_inc(scratch_out, 16)
            act.dma_start(mask_d[0:1].rearrange("(a b) -> a b", a=1), mask0[0:1, :]).then_inc(scratch_out, 16)

            def edge_rows_T(i, u):
                step = LONG * i + u
                act.wait_ge(e_xT, step + 1)
                nc.scalar.copy(xsT[:, :], pXs[:, :]).then_inc(xsT_ok, 1)
                nc.scalar.copy(xdT[:, :], pXdH[:, :]).then_inc(xdT_ok, 1)

            def node_rows_T(i, u, b):
                act.wait_ge(n_xT, 2 * (LONG * i + u) + b + 1)
                nc.scalar.copy(xnT[:, b, :], pXn[:, :]).then_inc(xnT_ok, 1)

            def node_relu(i, u, b):
                act.wait_ge(n_h, 2 * (LONG * i + u) + b + 1)
                nc.scalar.activation(hn[:, b, :], pHn[:, :], ACT.Relu, bias=c1c[:, :]).then_inc(hn_ok, 1)

            def root(i, u, b):
                act.wait_ge(var_ok, 3 * (LONG * i + u) + b + 1)
                nc.scalar.activation(std[:, b, :], mv[:, b, :, 1], ACT.Sqrt, bias=eps[:, :]).then_inc(std_ok, 1)

            def step_of(i, u, last=False):
                step = LONG * i + u
                j, v = i + (u + 1) // LONG, (u + 1) % LONG
                step_before = (i - 1, LONG - 1) if u == 0 else (i, u - 1)
                if isinstance(i, int) and step == 0:
                    step_before = None
                act.wait_ge(e_h1, step + 1)
                nc.scalar.activation(h1[:, :], pXdH[:, :], ACT.Relu, bias=b1c[:, :]).then_inc(h1_ok, 1)
                if step_before:
                    root(*step_before, 2)
                node_rows_T(i, u, 1)
                node_relu(i, u, 0)
                node_relu(i, u, 1)
                root(i, u, 0)
                act.wait_ge(e_h2, step + 1)
                nc.scalar.activation(h2[:, :], pMU[:, :], ACT.Relu, bias=c1e[:, :]).then_inc(h2_ok, 1)
                if not last:
                    edge_rows_T(j, v)
                    node_rows_T(j, v, 0)
                scatter_rows(i, u)
                if not isinstance(i, int) or LONG * i + u + RING < STEPS:
                    gather_rows(i + (u + RING) // LONG, (u + RING) % LONG)
                root(i, u, 1)

            edge_rows_T(0, 0)
            node_rows_T(0, 0, 0)
            act.wait_ge(weights_in, 16 * NW)
            act.wait_ge(tables_ok, 4)
            act.wait_ge(c1e_ok, 1)
            for u in range(LONG):
                step_of(0, u)
            with act.Fori(1, ROUNDS - 1) as i:
                for u in range(LONG):
                    step_of(i, u)
            for u in range(LONG):
                step_of(ROUNDS - 1, u)
            for u in range(LEFT):
                step_of(ROUNDS, u, last=(u == LEFT - 1))
            root(ROUNDS, LEFT - 1, 2)

            def late_rows(i, u):
                if not isinstance(i, int) or i > 0:
                    act.wait_ge(late_out[u], 16 * G * i)
                nc.scalar.copy(li[:, u, :], late_t[:, ds((RING * i + u) * G, G)]).then_inc(li_ok, 1)

            act.wait_ge(flag_ok, 2)
            late = act.value_load(flags[0:1, 1:2])
            with act.If(late > 0):
                for u in range(RING):
                    late_rows(0, u)
                with act.Fori(1, STEPS // RING) as i:
                    for u in range(RING):
                        late_rows(i, u)
                for u in range(STEPS % RING):
                    late_rows(STEPS // RING, u)

        @block.vector
        def _(dve):
            links = [0]

            def link(ins):
                links[0] += 1
                ins.then_inc(chain, 1)
                dve.wait_ge(chain, links[0])

            sort_links = [0]

            def sort_link(ins):
                sort_links[0] += 1
                ins.then_inc(sort_chain, 1)
                dve.wait_ge(sort_chain, sort_links[0])

            nc.vector.memset(ints[:, 0, CF, :], 0)
            nc.vector.memset(ints[:, 1, CF, :], SKIP)
            nc.vector.memset(ints[:, 2, CF, :], SKIP)
            nc.vector.memset(wrow[:, CF, :], 0.0).then_inc(padded, 1)
            nc.vector.memset(eps[:, :], EPS)
            nc.vector.memset(ones1[:, :], 1.0)
            nc.vector.memset(mask0[:, :], NEG)
            nc.vector.memset(ones[:, :], 1.0).then_inc(consts_ok, 1)

            def three_parts(parts, rest):
                for a, part in enumerate(parts):
                    link(nc.vector.tensor_copy(part, rest))
                    if a < 2:
                        link(nc.vector.tensor_tensor(rest, rest, part, ALU.subtract))

            dve.wait_ge(dst_in, 16 * 6)
            dve.wait_ge(consts_ok, 1)
            flat = [ints[:, k].rearrange("r c l -> r (c l)") for k in range(3)]
            wflat = wrow[:, :, :].rearrange("r c l -> r (c l)")

            def flag(k, which):
                link(nc.vector.tensor_reduce(flagp[:, k:k + 1], which, mybir.AxisListType.X, ALU.max))
                dve.nop(nofuse=True)
                dve.sem_inc(flag_in, 1)

            def flag_integer(k):
                dve.wait_ge(flag_sum, k + 1)
                nc.vector.tensor_copy(flags[0:1, k:k + 1], pHn[0:1, k:k + 1]).then_inc(flag_ok, 1)

            link(nc.vector.tensor_tensor(lastf[:, :], flat[2], flat[1], ALU.is_lt))
            flag(0, lastf[:, :])
            flag_integer(0)
            dve.wait_ge(flag_ok, 1)
            dve.wait_ge(src_in, 16 * 3)

            unsorted = dve.value_load(flags[0:1, 0:1])
            with dve.If(unsorted > 0):
                dve.wait_ge(edge_weight_in, 16 * 3)
                UNIT = 2.0 ** -16
                dve.wait_ge(iota_ok, 2)
                sort_link(nc.vector.memset(rank[:, :], 0.0))
                sort_link(nc.vector.tensor_copy(dstf[:, :], flat[1]))
                nc.vector.tensor_scalar(place[:, :], place_i[:, :], UNIT, None, ALU.mult)
                sort_link(nc.vector.tensor_scalar(chunk_pos[:, :], chunk[:, :], UNIT, None, ALU.mult))
                dve.nop(nofuse=True)
                dve.sem_inc(chunk_free, 1)
                with dve.Fori(0, E // CW) as c:
                    dve.wait_ge(chunk_in, 16 * (c + 1))
                    dve.nop(nofuse=True)
                    dve.sem_inc(counted, 1)
                    with dve.Fori(0, CH * P) as m:
                        dve.wait_ge(counted, c * (CH * P + 2) + m + 1)
                        nc.vector.scalar_tensor_tensor(out=before[:, :], in0=chunk[:, :],
                                                       scalar=dstf[:, ds(m, 1)], in1=chunk_pos[:, :],
                                                       op0=ALU.subtract, op1=ALU.add).then_inc(compared, 1)
                        dve.wait_ge(compared, c * (CH * P) + m + 1)
                        nc.vector.tensor_scalar(before[:, :], before[:, :], place[:, ds(m, 1)], None, ALU.is_lt,
                                                ALU.add, accum_out=count[:, ds(m, 1)]).then_inc(counted, 1)
                    dve.wait_ge(counted, (c + 1) * (CH * P + 2) - 1)
                    nc.vector.tensor_tensor(rank[:, :], rank[:, :], count[:, :], ALU.add)
                    nc.vector.tensor_scalar(place[:, :], place[:, :], -CW * UNIT, None, ALU.add).then_inc(counted, 1)
                    dve.wait_ge(counted, (c + 1) * (CH * P + 2))
                    dve.nop(nofuse=True)
                    dve.sem_inc(chunk_free, 1)
                sort_link(nc.vector.tensor_scalar(lastf[:, :], flat[1], float(SKIP), None, ALU.is_lt))
                sort_link(nc.vector.scalar_tensor_tensor(out=rank[:, :], in0=rank[:, :], scalar=float(-SKIP),
                                                         in1=lastf[:, :], op0=ALU.add, op1=ALU.mult))
                sort_link(nc.vector.tensor_scalar(rank[:, :], rank[:, :], float(SKIP), None, ALU.add))
                with dve.Fori(0, CH * P) as m:
                    dve.wait_ge(moved_free, m + 1)
                    nc.vector.tensor_copy(moved[:, 0:1], rank[:, ds(m, 1)])
                    nc.vector.tensor_copy(moved[:, 1:2], flat[0][:, ds(m, 1)])
                    nc.vector.tensor_copy(moved[:, 2:3], flat[1][:, ds(m, 1)])
                    nc.vector.tensor_copy(moved[:, 3:4].bitcast(f32), wflat[:, ds(m, 1)]).then_inc(moved_ok, 1)
                dve.wait_ge(sorted_in, 16 * 12)
                dve.nop(nofuse=True)

            nc.vector.tensor_copy(srcf[:, :], flat[0])
            nc.vector.tensor_scalar(dstf[:, :], flat[1], float(N - 1), None, ALU.min).then_inc(indices_ok, 1)
            link(nc.vector.tensor_tensor(lastf[:, :], flat[1], flat[2], ALU.not_equal))

            def tables(k, pair):
                for n, (t, bk) in enumerate(pair):
                    dve.wait_ge(tables_T, CH * (2 * k + n + 1))
                    nc.vector.tensor_copy(t[:, :], bk[:, 0:CH * P]).then_inc(tables_ok, 1)

            tables(0, ((src_t, pXs), (dst_t, pXdH)))
            dve.wait_ge(rows_in, 32)
            three_parts([part2[:, a] for a in range(3)], row2[:, :, :])
            dve.nop(nofuse=True)
            dve.sem_inc(parts_ok, 1)
            nc.vector.tensor_scalar(maskr[:, :, :].rearrange("r c l -> r (c l)"), lastf[:, :], NEG, None, ALU.mult)
            dve.wait_ge(edge_weight_in, 16 * 3)
            three_parts([wp[:, :, a, :] for a in range(3)], wrow[:, :, :])
            dve.nop(nofuse=True)
            dve.sem_inc(scratch_ok, 1)
            dve.wait_ge(iota_ok, 1)
            link(nc.vector.tensor_tensor(latef[:, :], flat[1], limit[:, :], ALU.is_ge))
            link(nc.vector.tensor_tensor(latef[:, :], latef[:, :], lastf[:, :], ALU.mult))
            nc.vector.tensor_tensor(nowf[:, :], lastf[:, :], latef[:, :], ALU.subtract)
            flag(1, latef[:, :])
            for t in (nowf, latef):
                link(nc.vector.scalar_tensor_tensor(out=t[:, :], in0=flat[1], scalar=float(-SKIP), in1=t[:, :],
                                                    op0=ALU.add, op1=ALU.mult))
                link(nc.vector.tensor_scalar(t[:, :], t[:, :], float(SKIP), None, ALU.add))
            dve.nop(nofuse=True)
            dve.sem_inc(indices_ok, 1)
            flag_integer(1)
            tables(1, ((now_t, pMU), (late_t, pXn)))
            dve.wait_ge(b2u_done, 1)
            dve.wait_ge(weights_in, 16 * NW)
            nc.vector.tensor_tensor(c1e[:, :], c1e[:, :], pZe[:, 0:1], ALU.add).then_inc(c1e_ok, 1)

            def running_max(i, u, first=False):
                step = LONG * i + u
                dve.wait_ge(e_msg, step + 1)
                if not first:
                    dve.wait_ge(agg_ok, step)
                nc.vector.tensor_tensor_scan(agg[:, u % 2, :], mk[:, u % RING, :], pMU[:, :],
                                             NEG if first else agg[:, (u + 1) % 2, EB - 1:EB],
                                             ALU.add, ALU.max).then_inc(agg_ok, 1)

            def result(u, b):
                k = u % RING
                if b < 2:
                    return on[:, k, b * G:(b + 1) * G, :], pZn[b], xn[:, k, b * G:(b + 1) * G, :]
                return oe[:, u], pZe, xd[:, k]

            def residual(i, u, b):
                z, bk, rows = result(u, b)
                batch = 3 * (LONG * i + u) + b
                if b < 2:
                    dve.wait_ge(n_z, 2 * (LONG * i + u) + b + 1)
                else:
                    dve.wait_ge(e_z, LONG * i + u + 1)
                turn = 2 * i + u // RING
                if b == 0 and (not isinstance(i, int) or turn > 0):
                    dve.wait_ge(on_out[u % RING], 16 * turn)
                if b == 2 and (not isinstance(i, int) or i > 0):
                    dve.wait_ge(oe_out[u], 16 * i)
                    dve.wait_ge(scattered[u], 16 * G * i)
                nc.vector.tensor_tensor(z, bk[:, :].rearrange("p (g d) -> p g d", g=G), rows, ALU.add
                                        ).then_inc(added, 1)
                dve.wait_ge(added, batch + 1)
                for g in range(G):
                    last = nc.vector.bn_stats(stats[:, b, g, :], z[:, g, :])
                last.then_inc(stat_ok, 1)
                dve.wait_ge(stat_ok, batch + 1)
                dve.nop(nofuse=True)
                for g in range(G):
                    last = nc.vector.bn_aggr(mv[:, b, g, :], stats[:, b, g, :])
                last.then_inc(var_ok, 1)

            def normalise(i, u, b):
                z, _, _ = result(u, b)
                batch = 3 * (LONG * i + u) + b
                dve.wait_ge(std_ok, batch + 1)
                nc.vector.reciprocal(rstd[:, b, :], std[:, b, :]).then_inc(rstd_ok, 1)
                dve.wait_ge(rstd_ok, batch + 1)
                for g in range(G):
                    last = nc.vector.tensor_scalar(z[:, g, :], z[:, g, :], mv[:, b, g, 0:1], rstd[:, b, g:g + 1],
                                                   ALU.subtract, ALU.mult)
                last.then_inc(norm_ok, 1)

            def step_of(i, u, first=False):
                running_max(i, u, first)
                residual(i, u, 0)
                residual(i, u, 1)
                normalise(i, u, 0)
                residual(i, u, 2)
                normalise(i, u, 1)
                normalise(i, u, 2)

            for u in range(LONG):
                step_of(0, u, first=(u == 0))
            with dve.Fori(1, ROUNDS) as i:
                for u in range(LONG):
                    step_of(i, u)
            for u in range(LEFT):
                step_of(ROUNDS, u)


_INS = ['x', 'src', 'dst', 'edge_weight', 'L0_gnn_W1', 'L0_gnn_b1', 'L0_gnn_W2', 'L0_gnn_b2',
        'L0_gnn_U1', 'L0_gnn_c1', 'L0_gnn_U2', 'L0_gnn_c2']


def kernel(**inputs):
    import concourse.bacc as _bacc
    from concourse.bass_utils import run_bass_kernel_spmd as _run

    nc = _bacc.Bacc("TRN2", target_bir_lowering=False, num_devices=1)
    arrays, args = {}, []
    for name in _INS:
        a = np.ascontiguousarray(inputs[name])
        arrays[f"in_{name}_dram"] = a
        args.append(nc.dram_tensor(f"in_{name}_dram", a.shape, mybir.dt.from_np(a.dtype), kind="ExternalInput").ap())
    x = inputs['x']
    args.append(nc.dram_tensor("out_0_dram", x.shape, mybir.dt.float32, kind="ExternalOutput").ap())
    build(nc, *args)
    r = _run(nc, [arrays], core_ids=[0])
    return r.results[0]["out_0_dram"]
```
